# Optimizing a Trainium2 kernel written in Bass

```python
import numpy as np
import jax
import jax.numpy as jnp

def _softmax(x, axis=-1):
    return jax.nn.softmax(x, axis=axis)

def _gelu(x):
    return jax.nn.gelu(x, approximate=True)

def _silu(x):
    return jax.nn.silu(x)

def _sigmoid(x):
    return jax.nn.sigmoid(x)

def _layernorm(x, axis=-1, eps=1e-05):
    m = jnp.mean(x, axis=axis, keepdims=True)
    v = jnp.var(x, axis=axis, keepdims=True)
    return (x - m) / jnp.sqrt(v + eps)

def _scatter_add(tgt, idx, src, axis=0):
    return tgt.at[idx].add(src)

def _segment_sum(src, seg, n):
    return jax.ops.segment_sum(src, seg, n)
kernel_name = 'mk_rec_standalone_d1_rec_r8_169635'

def setup_inputs(seed: int=0):
    np.random.seed(seed)
    _w = jnp.asarray

    def _rec_inputs():
        import jax
        import jax.numpy as jnp
        _rk = jax.random.key(seed)
        r_dense = -0.00338568 + 1.0005 * jax.random.normal(jax.random.fold_in(_rk, 1), (512, 13), jnp.float32)
        r_indices = jnp.stack([jax.random.randint(jax.random.fold_in(jax.random.fold_in(_rk, 2), 0), (512,), 13, 99986, jnp.int32), jax.random.randint(jax.random.fold_in(jax.random.fold_in(_rk, 2), 1), (512,), 4, 99994, jnp.int32), jax.random.randint(jax.random.fold_in(jax.random.fold_in(_rk, 2), 2), (512,), 0, 99999, jnp.int32), jax.random.randint(jax.random.fold_in(jax.random.fold_in(_rk, 2), 3), (512,), 0, 99998, jnp.int32), jax.random.randint(jax.random.fold_in(jax.random.fold_in(_rk, 2), 4), (512,), 4, 99998, jnp.int32), jax.random.randint(jax.random.fold_in(jax.random.fold_in(_rk, 2), 5), (512,), 1, 99989, jnp.int32), jax.random.randint(jax.random.fold_in(jax.random.fold_in(_rk, 2), 6), (512,), 2, 99993, jnp.int32), jax.random.randint(jax.random.fold_in(jax.random.fold_in(_rk, 2), 7), (512,), 3, 99995, jnp.int32), jax.random.randint(jax.random.fold_in(jax.random.fold_in(_rk, 2), 8), (512,), 0, 99993, jnp.int32), jax.random.randint(jax.random.fold_in(jax.random.fold_in(_rk, 2), 9), (512,), 6, 99999, jnp.int32), jax.random.randint(jax.random.fold_in(jax.random.fold_in(_rk, 2), 10), (512,), 4, 12500, jnp.int32), jax.random.randint(jax.random.fold_in(jax.random.fold_in(_rk, 2), 11), (512,), 18, 99998, jnp.int32), jax.random.randint(jax.random.fold_in(jax.random.fold_in(_rk, 2), 12), (512,), 0, 99991, jnp.int32), jax.random.randint(jax.random.fold_in(jax.random.fold_in(_rk, 2), 13), (512,), 8, 99999, jnp.int32), jax.random.randint(jax.random.fold_in(jax.random.fold_in(_rk, 2), 14), (512,), 0, 99993, jnp.int32), jax.random.randint(jax.random.fold_in(jax.random.fold_in(_rk, 2), 15), (512,), 0, 99990, jnp.int32), jax.random.randint(jax.random.fold_in(jax.random.fold_in(_rk, 2), 16), (512,), 2, 99998, jnp.int32), jax.random.randint(jax.random.fold_in(jax.random.fold_in(_rk, 2), 17), (512,), 7, 99995, jnp.int32), jax.random.randint(jax.random.fold_in(jax.random.fold_in(_rk, 2), 18), (512,), 2, 12500, jnp.int32), jax.random.randint(jax.random.fold_in(jax.random.fold_in(_rk, 2), 19), (512,), 5, 99999, jnp.int32), jax.random.randint(jax.random.fold_in(jax.random.fold_in(_rk, 2), 20), (512,), 13, 99999, jnp.int32), jax.random.randint(jax.random.fold_in(jax.random.fold_in(_rk, 2), 21), (512,), 2, 12500, jnp.int32), jax.random.randint(jax.random.fold_in(jax.random.fold_in(_rk, 2), 22), (512,), 2, 99998, jnp.int32), jax.random.randint(jax.random.fold_in(jax.random.fold_in(_rk, 2), 23), (512,), 13, 99995, jnp.int32), jax.random.randint(jax.random.fold_in(jax.random.fold_in(_rk, 2), 24), (512,), 1, 99978, jnp.int32), jax.random.randint(jax.random.fold_in(jax.random.fold_in(_rk, 2), 25), (512,), 6, 99995, jnp.int32)], axis=0)
        return (r_dense, r_indices)
    r_dense, r_indices = _rec_inputs()

    def _L0_rec_setup():
        import jax, jax.numpy as jnp
        import numpy as np
        B = 2048
        D_DENSE = 13
        N_SPARSE = 26
        EMB = 128
        VOCAB = 12500
        LN_BOT = [13, 512, 256, 128]
        LN_TOP = [479, 1024, 1024, 512, 256, 1]
        N_FEAT = N_SPARSE + 1
        TRIU_I, TRIU_J = np.triu_indices(N_FEAT, k=1)

        def _init_mlp(key, ln, prefix, out):
            for i in range(len(ln) - 1):
                n, m = (ln[i], ln[i + 1])
                kw, kb = jax.random.split(jax.random.fold_in(key, i))
                out[f'{prefix}w{i}'] = jax.random.normal(kw, (n, m), jnp.float32) * np.sqrt(2.0 / (m + n))
                out[f'{prefix}b{i}'] = jax.random.normal(kb, (m,), jnp.float32) * np.sqrt(1.0 / m)

        def _dlrm_forward(dense, indices, emb_tables, bot_params, top_params):
            x = dense
            for w, b in bot_params:
                x = jax.nn.relu(x @ w + b)
            feats = jax.vmap(lambda tbl, idx: tbl[idx])(emb_tables, indices)
            T = jnp.concatenate([x[None], feats], axis=0).transpose(1, 0, 2)
            Z = jnp.einsum('bie,bje->bij', T, T)
            R = Z[:, TRIU_I, TRIU_J]
            x = jnp.concatenate([x, R], axis=1)
            n_top = len(top_params)
            for i, (w, b) in enumerate(top_params):
                y = x @ w + b
                x = jax.nn.sigmoid(y) if i == n_top - 1 else jax.nn.relu(y)
            return x
        key = jax.random.key(seed)
        kd, ki, ke, kbot, ktop = jax.random.split(key, 5)
        inp = {'dense': jax.random.normal(kd, (B, D_DENSE), jnp.float32), 'indices': jax.random.randint(ki, (N_SPARSE, B), 0, VOCAB, dtype=jnp.int32), 'emb_tables': jax.random.normal(ke, (N_SPARSE, VOCAB, EMB), jnp.float32) * 0.01}
        _init_mlp(kbot, LN_BOT, 'b', inp)
        _init_mlp(ktop, LN_TOP, 't', inp)
        return inp
    _L0_rec_all = _L0_rec_setup()
    _L0_rec_in = {k: v for k, v in _L0_rec_all.items() if k in ('emb_tables', 'bw0', 'bb0', 'bw1', 'bb1', 'bw2', 'bb2', 'tw0', 'tb0', 'tw1', 'tb1', 'tw2', 'tb2', 'tw3', 'tb3', 'tw4', 'tb4')}
    del _L0_rec_all
    return {'r_dense': r_dense, 'r_indices': r_indices, 'L0_rec_emb_tables': _L0_rec_in['emb_tables'], 'L0_rec_bw0': _L0_rec_in['bw0'], 'L0_rec_bb0': _L0_rec_in['bb0'], 'L0_rec_bw1': _L0_rec_in['bw1'], 'L0_rec_bb1': _L0_rec_in['bb1'], 'L0_rec_bw2': _L0_rec_in['bw2'], 'L0_rec_bb2': _L0_rec_in['bb2'], 'L0_rec_tw0': _L0_rec_in['tw0'], 'L0_rec_tb0': _L0_rec_in['tb0'], 'L0_rec_tw1': _L0_rec_in['tw1'], 'L0_rec_tb1': _L0_rec_in['tb1'], 'L0_rec_tw2': _L0_rec_in['tw2'], 'L0_rec_tb2': _L0_rec_in['tb2'], 'L0_rec_tw3': _L0_rec_in['tw3'], 'L0_rec_tb3': _L0_rec_in['tb3'], 'L0_rec_tw4': _L0_rec_in['tw4'], 'L0_rec_tb4': _L0_rec_in['tb4']}

def reference(r_dense, r_indices, L0_rec_emb_tables, L0_rec_bw0, L0_rec_bb0, L0_rec_bw1, L0_rec_bb1, L0_rec_bw2, L0_rec_bb2, L0_rec_tw0, L0_rec_tb0, L0_rec_tw1, L0_rec_tb1, L0_rec_tw2, L0_rec_tb2, L0_rec_tw3, L0_rec_tb3, L0_rec_tw4, L0_rec_tb4):
    import jax
    import jax.numpy as jnp

    def _L0_rec_ref(dense, indices, emb_tables, bw0, bb0, bw1, bb1, bw2, bb2, tw0, tb0, tw1, tb1, tw2, tb2, tw3, tb3, tw4, tb4):
        import jax, jax.numpy as jnp
        import numpy as np
        B = 2048
        D_DENSE = 13
        N_SPARSE = 26
        EMB = 128
        VOCAB = 12500
        LN_BOT = [13, 512, 256, 128]
        LN_TOP = [479, 1024, 1024, 512, 256, 1]
        N_FEAT = N_SPARSE + 1
        TRIU_I, TRIU_J = np.triu_indices(N_FEAT, k=1)

        def _init_mlp(key, ln, prefix, out):
            for i in range(len(ln) - 1):
                n, m = (ln[i], ln[i + 1])
                kw, kb = jax.random.split(jax.random.fold_in(key, i))
                out[f'{prefix}w{i}'] = jax.random.normal(kw, (n, m), jnp.float32) * np.sqrt(2.0 / (m + n))
                out[f'{prefix}b{i}'] = jax.random.normal(kb, (m,), jnp.float32) * np.sqrt(1.0 / m)

        def _dlrm_forward(dense, indices, emb_tables, bot_params, top_params):
            x = dense
            for w, b in bot_params:
                x = jax.nn.relu(x @ w + b)
            feats = jax.vmap(lambda tbl, idx: tbl[idx])(emb_tables, indices)
            T = jnp.concatenate([x[None], feats], axis=0).transpose(1, 0, 2)
            Z = jnp.einsum('bie,bje->bij', T, T)
            R = Z[:, TRIU_I, TRIU_J]
            x = jnp.concatenate([x, R], axis=1)
            n_top = len(top_params)
            for i, (w, b) in enumerate(top_params):
                y = x @ w + b
                x = jax.nn.sigmoid(y) if i == n_top - 1 else jax.nn.relu(y)
            return x
        bot = [(bw0, bb0), (bw1, bb1), (bw2, bb2)]
        top = [(tw0, tb0), (tw1, tb1), (tw2, tb2), (tw3, tb3), (tw4, tb4)]
        return _dlrm_forward(dense, indices, emb_tables, bot, top)
    y = _L0_rec_ref(r_dense, r_indices, L0_rec_emb_tables, L0_rec_bw0, L0_rec_bb0, L0_rec_bw1, L0_rec_bb1, L0_rec_bw2, L0_rec_bb2, L0_rec_tw0, L0_rec_tb0, L0_rec_tw1, L0_rec_tb1, L0_rec_tw2, L0_rec_tb2, L0_rec_tw3, L0_rec_tb3, L0_rec_tw4, L0_rec_tb4)
    return y

_drawn_inputs = setup_inputs


def setup_inputs(seed=0):
    import zlib

    import numpy as np

    out = dict(_drawn_inputs(seed))
    spreads = {}
    factors = {'r_dense': 8.0,
     'L0_rec_emb_tables': 8.0,
     'L0_rec_bw0': 8.0,
     'L0_rec_bb0': 8.0,
     'L0_rec_bw1': 8.0,
     'L0_rec_bb1': 8.0,
     'L0_rec_bw2': 8.0,
     'L0_rec_bb2': 8.0,
     'L0_rec_tw0': 5.565,
     'L0_rec_tb0': 8.0,
     'L0_rec_tw1': 8.0,
     'L0_rec_tb1': 8.0,
     'L0_rec_tw2': 6.25,
     'L0_rec_tw3': 4.335,
     'L0_rec_tb3': 8.0,
     'L0_rec_tw4': 6.343}
    for name, (base, spread) in spreads.items():
        noise = np.random.default_rng([zlib.crc32(name.encode()), seed]).standard_normal(out[name].shape)
        drawn = base * np.exp(spread * noise) if base else spread * noise
        out[name] = jnp.asarray(drawn.astype(out[name].dtype))
    for name, factor in factors.items():
        out[name] = (out[name] * factor).astype(out[name].dtype)
    return out
```

```python
from contextlib import ExitStack

import concourse.bass as bass
from concourse import mybir

ALU = mybir.AluOpType
ACT = mybir.ActivationFunctionType
F32 = mybir.dt.float32
F32R = mybir.dt.float32r
I32 = mybir.dt.int32
U32 = mybir.dt.uint32

P = 128
BANK = 512
GROUPS = (4, 3, 3, 3) * 2
SLOTS = 4
DMA = 16


def pair_rows(n_feat, first_row):
    table = [[first_row] * 3 for _ in range(P)]

    def row(i, j):
        a, b = min(i, j % n_feat), max(i, j % n_feat)
        return first_row + a * n_feat - a * (a + 1) // 2 + b - a - 1

    for q in range(4):
        for i in range(n_feat):
            for t in range(3):
                table[32 * q + i][t] = row(i, i + 1 + 3 * q + t)
    for t in range(3):
        for r in range(5):
            table[n_feat + r][t] = row(5 * t + r, 5 * t + r + 13)
        for r in range(4):
            table[32 + n_feat + r][t] = row(15 + 4 * t + r, 15 + 4 * t + r + 13)
    return table


def dlrm_program(nc, dense, indices, tables, bw0, bb0, bw1, bb1, bw2, bb2,
                 tw0, tb0, tw1, tb1, tw2, tb2, tw3, tb3, tw4, tb4, pair_row, table_base, out):
    B, n_dense = dense.shape
    n_tab, vocab, emb = tables.shape
    CHUNKS = B // P
    NF = n_tab + 1
    FS = NF + 1
    n1, n2, n3, n4 = tw0.shape[1], tw1.shape[1], tw2.shape[1], tw3.shape[1]
    U0, U1 = bw0.shape[1], bw1.shape[1]
    K1, K2, K3 = n1 // P, n2 // P, n3 // P
    NG = len(GROUPS)
    FIRST = [sum(GROUPS[:g]) for g in range(NG)]
    SLOT0 = [sum(GROUPS[:s]) for s in range(SLOTS)]
    ZS = 16
    ZR = P // ZS
    JA = 14
    JW = NF + 13
    assert (emb, NF, n1, n2, n3, n4) == (P, 27, 1024, 1024, 512, 256) and sum(GROUPS) == n_tab

    with ExitStack() as ctx:
        def sem(name):
            return ctx.enter_context(nc.semaphore(name))

        place = [(nc.sbuf_base + 31) // 32 * 32]

        def at(name, shape, dt, offset):
            return nc.alloc_sbuf_tensor_at(name, shape, dt, offset=offset)

        def new(name, shape, dt=F32):
            size = 4
            for n in shape[1:]:
                size *= n
            offset = place[0]
            place[0] += (size + 31) // 32 * 32
            return at(name, shape, dt, offset), offset

        def parts(name, shape):
            hi, hi_at = new(name + "_hi", shape, F32R)
            lo, lo_at = new(name + "_lo", shape, F32R)
            return hi, lo, at(name + "_raw", shape, F32, lo_at), hi_at, lo_at

        w1h, w1l, w1raw, _, _ = parts("w1", [P, 3, n1])
        w2h, w2l, w2raw, _, _ = parts("w2", [P, K1, n2])
        w3h, w3l, w3raw, w3_at, _ = parts("w3", [P, K2, n3])
        w4h, w4l, w4raw, _, _ = parts("w4", [P, K3, n4])
        fh, _ = new("feat_hi", [P, P, FS], F32R)
        fl, _ = new("feat_lo", [P, P, FS], F32R)
        rh, _ = new("pair_hi", [P, 3, P], F32R)
        rl, _ = new("pair_lo", [P, 3, P], F32R)
        rraw = rl[:, :, :].bitcast(F32)
        h1h, h1_at = new("h1_hi", [P, K1, P], F32R)
        h1l, h1l_at = new("h1_lo", [P, K1, P], F32R)
        h2h, _ = new("h2_hi", [P, K2, P], F32R)
        h2l, _ = new("h2_lo", [P, K2, P], F32R)
        gat, _ = new("gathered", [P, sum(GROUPS[:SLOTS]), emb])
        zs, zs_at = new("gram", [P, JA, P])
        xpart, _ = new("xpart", [P, n1])
        sums, _ = new("sums", [P, n1])
        b1, _ = new("b1", [P, n2])
        b2, _ = new("b2", [P, n3])
        b3, _ = new("b3", [P, n4])
        w5, _ = new("w5", [P, n4])
        b5, _ = new("b5", [P, 1])
        xT, _ = new("xT", [P, B])
        ident, _ = new("ident", [P, P])
        rows, _ = new("rows", [P, CHUNKS * n_tab], U32)
        prow, _ = new("prow", [P, 3], U32)
        tbase, _ = new("tbase", [n_tab, 1])
        dotc, _ = new("dotc", [P, 1])
        logit, _ = new("logit", [P, CHUNKS])
        prob, _ = new("prob", [P, CHUNKS])
        assert place[0] <= nc.sbuf_usable_end, place[0] - nc.sbuf_usable_end
        h3h = at("h3_hi", [P, K3, P], F32R, h1_at)
        h3l = at("h3_lo", [P, K3, P], F32R, h1l_at)
        w0h = at("w0_hi", [P, n1], F32R, h1_at)
        w0l = at("w0_lo", [P, n1], F32R, h1l_at)
        w0raw = at("w0_raw", [P, n1], F32, h1l_at)
        idx_i = at("idx_i", [n_tab, B], I32, zs_at)
        idx_n = at("idx_n", [n_tab, B], F32, zs_at + 4 * B)
        idx_f = at("idx_f", [n_tab, B], F32, zs_at + 8 * B)
        early = [w3_at]

        def new_early(name, shape, dt=F32):
            size = 4
            for n in shape[1:]:
                size *= n
            early[0] += (size + 31) // 32 * 32
            return at(name, shape, dt, early[0] - (size + 31) // 32 * 32)

        bot0 = new_early("bot0", [P, U0 // P, B])
        bot1 = new_early("bot1", [P, U1 // P, B])
        bw0s = new_early("bw0s", [n_dense, U0])
        bw1s = new_early("bw1s", [P, U0 // P, U1])
        bw2s = new_early("bw2s", [P, U1 // P, emb])
        den = new_early("den", [P, CHUNKS * n_dense])
        denT = new_early("denT", [n_dense, B])
        brow = new_early("brow", [7, P])
        bcol = new_early("bcol", [P, 7])
        b0 = new_early("b0", [P, n1])
        xh = new_early("x_hi", [P, B], F32R)
        xl = new_early("x_lo", [P, B], F32R)
        assert early[0] <= w3_at + 2 * 4 * K2 * n3

        feat_ps = [ctx.enter_context(nc.psum_tensor(f"feat_ps{i}", [P, BANK], F32)) for i in range(2)]
        gram_ps = [ctx.enter_context(nc.psum_tensor(f"gram_ps{i}", [P, BANK], F32)) for i in range(2)]
        sum_ps = [ctx.enter_context(nc.psum_tensor(f"sum_ps{i}", [P, BANK], F32)) for i in range(2)]
        turn_ps = [ctx.enter_context(nc.psum_tensor(f"turn_ps{i}", [P, BANK], F32)) for i in range(2)]

        GRAM = NF * (JW + 1) * P
        gram_dram = nc.dram_tensor("gram_dram", (CHUNKS * GRAM,), F32, kind="Internal").ap()
        xpart_dram = nc.dram_tensor("xpart_dram", (CHUNKS * P * n1,), F32, kind="Internal").ap()

        idx_in, den_in, bias_in, bot_w_in = sem("idx_in"), sem("den_in"), sem("bias_in"), sem("bot_w_in")
        prow_in, b0_in, tail_in = sem("prow_in"), sem("b0_in"), sem("tail_in")
        w_in = [sem(f"w_in{i}") for i in range(9)]
        w_hi, w_lo = sem("w_hi"), sem("w_lo")
        ident_step, ident_ready = sem("ident_step"), sem("ident_ready")
        chain = sem("vector_chain")
        cleared = sem("cleared")
        early_turned, bcol_ready = sem("early_turned"), sem("bcol_ready")
        bot_full, bot_read = sem("bot_full"), sem("bot_read")
        x_hi, x_lo = sem("x_hi_ready"), sem("x_lo_ready")
        xp_full = sem("xp_full")
        xp_stored = [sem(f"xp_stored{i}") for i in range(2)]
        xp_loaded = sem("xp_loaded")
        slot_loaded = [sem(f"slot_loaded{s}") for s in range(SLOTS)]
        turned = sem("features_turned")
        feat_hi, feat_lo = sem("feat_hi_ready"), sem("feat_lo_ready")
        gram_done = sem("gram_done")
        gram_even, gram_odd = sem("gram_even"), sem("gram_odd")
        gram_stored, pair_loaded = sem("gram_stored"), sem("pair_loaded")
        pair_hi, pair_lo = sem("pair_hi_ready"), sem("pair_lo_ready")
        sum_full = [sem(f"sum_full{i}") for i in range(2)]
        sum_read = [sem(f"sum_read{i}") for i in range(2)]
        turn_full = [sem(f"turn_full{i}") for i in range(2)]
        turn_hi = [sem(f"turn_hi{i}") for i in range(2)]
        turn_lo = [sem(f"turn_lo{i}") for i in range(2)]
        dot_done, logit_done, prob_done, out_done = (
            sem("dot_done"), sem("logit_done"), sem("prob_done"), sem("out_done"))

        W0, W2A, W1, W3A, W4 = 0, 1, 5, 6, 8
        piece = [(w0h[:, :], w0l[:, :], w0raw[:, :])]
        piece += [(w2h[:, 2 * i:2 * i + 2, :], w2l[:, 2 * i:2 * i + 2, :], w2raw[:, 2 * i:2 * i + 2, :]) for i in range(4)]
        piece += [(w1h[:, :, :], w1l[:, :, :], w1raw[:, :, :])]
        piece += [(w3h[:, 4 * i:4 * i + 4, :], w3l[:, 4 * i:4 * i + 4, :], w3raw[:, 4 * i:4 * i + 4, :]) for i in range(2)]
        piece += [(w4h[:, :, :], w4l[:, :, :], w4raw[:, :, :])]

        block = ctx.enter_context(nc.Block())

        @block.gpsimd
        def _(pool):
            pool.memset(ident[:, :], 0.0).then_inc(ident_step, 1)
            pool.wait_ge(ident_step, 1)
            pool.affine_select(out=ident[:, :], in_=ident[:, :], compare_op=ALU.not_equal, fill=1.0,
                               base=0, pattern=[[-1, P]], channel_multiplier=1).then_inc(ident_ready, 1)
            pool.wait_ge(turn_lo[0], 1)
            all_rows = tables.rearrange("t v e -> (t v) e")
            for c in range(CHUNKS):
                for g, size in enumerate(GROUPS):
                    s, fill = g % SLOTS, NG // SLOTS * c + g // SLOTS
                    if fill > 0:
                        pool.wait_ge(turned, NG * c + g - SLOTS + 1)
                    for k in range(size):
                        col = c * n_tab + FIRST[g] + k
                        pool.indirect_dma_start(
                            out=gat[:, SLOT0[s] + k, :], out_offset=None, in_=all_rows,
                            in_offset=bass.IndirectOffsetOnAxis(ap=rows[:, col:col + 1], axis=0),
                        ).then_inc(slot_loaded[s], DMA)
                if c == 0:
                    pool.wait_ge(prow_in, DMA)
                    for t in range(3):
                        pool.indirect_dma_start(
                            out=w1raw[:, t, :], out_offset=None, in_=tw0,
                            in_offset=bass.IndirectOffsetOnAxis(ap=prow[:, t:t + 1], axis=0),
                        ).then_inc(w_in[W1], DMA)

        @block.sync
        def _(sp):
            sp.dma_start(idx_i[:, :], indices).then_inc(idx_in, DMA)
            sp.dma_start(tbase[:, :], table_base).then_inc(idx_in, DMA)
            sp.dma_start(den[:, :], dense.rearrange("(p c) k -> p (c k)", c=CHUNKS)).then_inc(den_in, DMA)
            sp.dma_start(bw0s[:, :], bw0).then_inc(bot_w_in, DMA)
            sp.dma_start(brow[0:4, :], bb0.rearrange("(m p) -> m p", p=P)).then_inc(bias_in, DMA)
            sp.dma_start(brow[4:6, :], bb1.rearrange("(m p) -> m p", p=P)).then_inc(bias_in, DMA)
            sp.dma_start(brow[6:7, :], bb2.rearrange("(m p) -> m p", p=P)).then_inc(bias_in, DMA)
            sp.dma_start(bw1s[:, :, :], bw1.rearrange("(k p) n -> p k n", p=P)).then_inc(bot_w_in, DMA)
            sp.dma_start(bw2s[:, :, :], bw2.rearrange("(k p) n -> p k n", p=P)).then_inc(bot_w_in, DMA)
            sp.dma_start(w0raw[:, :], tw0[0:P, :]).then_inc(w_in[W0], DMA)
            sp.dma_start(b0[:, :], tb0.partition_broadcast(P)).then_inc(b0_in, DMA)
            sp.dma_start(prow[:, :], pair_row).then_inc(prow_in, DMA)
            w2_rows = tw1.rearrange("(k p) n -> p k n", p=P)
            for i in range(4):
                sp.dma_start(w2raw[:, 2 * i:2 * i + 2, :], w2_rows[:, 2 * i:2 * i + 2, :]).then_inc(w_in[W2A + i], DMA)
            sp.dma_start(w4raw[:, :, :], tw3.rearrange("(k p) n -> p k n", p=P)).then_inc(w_in[W4], DMA)
            sp.dma_start(b1[:, :], tb1.partition_broadcast(P)).then_inc(tail_in, DMA)
            sp.dma_start(b2[:, :], tb2.partition_broadcast(P)).then_inc(tail_in, DMA)
            sp.dma_start(b3[:, :], tb3.partition_broadcast(P)).then_inc(tail_in, DMA)
            sp.dma_start(w5[:, :], tw4.rearrange("n o -> (n o)").partition_broadcast(P)).then_inc(tail_in, DMA)
            sp.dma_start(b5[:, :], tb4.partition_broadcast(P)).then_inc(tail_in, DMA)
            for c in range(CHUNKS):
                sp.wait_ge(sum_read[0], c + 1)
                sp.wait_ge(sum_read[1], c + 1)
                stage = (sums, xpart)[c % 2]
                sp.dma_start(xpart_dram[c * P * n1:(c + 1) * P * n1].rearrange("(p n) -> p n", p=P), stage[:, :]).then_inc(xp_stored[c % 2], DMA)
            w3_rows = tw2.rearrange("(k p) n -> p k n", p=P)
            for i in range(2):
                sp.dma_start(w3raw[:, 4 * i:4 * i + 4, :], w3_rows[:, 4 * i:4 * i + 4, :]).then_inc(w_in[W3A + i], DMA)
            sp.wait_ge(xp_stored[0], DMA * (CHUNKS // 2))
            sp.wait_ge(xp_stored[1], DMA * (CHUNKS // 2))
            sp.dma_start(xpart[:, :], xpart_dram[0:P * n1].rearrange("(p n) -> p n", p=P)).then_inc(xp_loaded, DMA)

            def pairs_through_dram(start, copied, stored):
                flat = gram_dram[bass.ds(start, GRAM)]
                by_row = flat[0:NF * JW * P].rearrange("(i j b) -> i j b", i=NF, j=JW)
                skewed = flat.rearrange("(i j b) -> i j b", i=NF, j=JW + 1)
                sp.wait_ge(gram_even, copied)
                sp.wait_ge(gram_odd, copied)
                sp.dma_start(by_row[:, JA:NF, :], zs[32:32 + NF, 0:NF - JA, :]).then_inc(gram_stored, DMA)
                sp.dma_start(by_row[0:13, 1:JA, :], zs[0:13, 1:JA, :]).then_inc(gram_stored, DMA)
                sp.dma_start(by_row[14:NF, NF:JW, :], zs[14:NF, 0:13, :]).then_inc(gram_stored, DMA)
                sp.wait_ge(gram_stored, stored)
                for q in range(4):
                    sp.dma_start(rraw[32 * q:32 * q + NF, :, :],
                                 skewed[:, 1 + 3 * q:4 + 3 * q, :]).then_inc(pair_loaded, DMA)
                far = skewed[:, 13, :]
                sp.dma_start(rraw[NF:NF + 5, :, :],
                             far[0:15, :].rearrange("(t r) b -> r t b", t=3)).then_inc(pair_loaded, DMA)
                sp.dma_start(rraw[32 + NF:32 + NF + 4, :, :],
                             far[15:NF, :].rearrange("(t r) b -> r t b", t=3)).then_inc(pair_loaded, DMA)

            sp.wait_ge(cleared, 3)
            pairs_through_dram(0, ZR, 3 * DMA)
            with sp.Fori(0, CHUNKS - 1) as c:
                shared = sp.snap(3 * c + CHUNKS + 1)
                copied = sp.snap(ZR * c + 2 * ZR)
                stored = sp.snap(3 * DMA * c + 6 * DMA)
                xpart_at = sp.snap((c + 1) * (P * n1))
                gram_at = sp.snap((c + 1) * GRAM)
                sp.wait_ge(sum_read[0], shared)
                sp.wait_ge(sum_read[1], shared)
                sp.dma_start(xpart[:, :], xpart_dram[bass.ds(xpart_at, P * n1)].rearrange("(p n) -> p n", p=P)).then_inc(xp_loaded, DMA)
                pairs_through_dram(gram_at, copied, stored)
            sp.wait_ge(prob_done, 1)
            sp.dma_start(out.rearrange("(p c) o -> p (c o)", c=CHUNKS), prob[:, :]).then_inc(out_done, DMA)
            sp.wait_ge(out_done, DMA)

        @block.scalar
        def _(act):
            def cut(i):
                act.wait_ge(w_in[i], 3 * DMA if i == W1 else DMA)
                act.activation(piece[i][0], piece[i][2], ACT.Copy).then_inc(w_hi, 1)

            def bottom_feature(c):
                act.wait_ge(gram_done, ZR * c)
                act.activation(fh[:, :, 0], xT[:, bass.ds(c * P, P)], ACT.Copy).then_inc(feat_hi, 1)

            def features(c, g):
                n = GROUPS[g]
                act.wait_ge(turned, NG * c + g + 1)
                act.activation(fh[:, :, 1 + FIRST[g]:1 + FIRST[g] + n],
                               feat_ps[g % 2][:, 0:n * P].rearrange("p (f b) -> p b f", f=n),
                               ACT.Copy).then_inc(feat_hi, 1)

            def gram_out(c):
                act.wait_ge(gram_stored, 3 * DMA * c)
                for r in range(0, ZR, 2):
                    act.wait_ge(gram_done, ZR * c + r + 1)
                    table = gram_ps[0][0:NF, 0:ZS * FS].rearrange("p (s j) -> p j s", s=ZS)
                    act.activation(zs[0:NF, 0:JA, r * ZS:(r + 1) * ZS], table[:, 0:JA, :],
                                   ACT.Copy).then_inc(gram_even, 1)
                    act.activation(zs[32:32 + NF, 0:NF - JA, r * ZS:(r + 1) * ZS], table[:, JA:NF, :],
                                   ACT.Copy).then_inc(gram_even, 1)

            def pairs(c):
                act.wait_ge(pair_loaded, 6 * DMA * (c + 1))
                act.activation(rh[:, :, :], rraw[:, :, :], ACT.Copy).then_inc(pair_hi, 1)

            def relu_hi(dst, half, count):
                act.wait_ge(turn_full[half], count)
                act.activation(dst, turn_ps[half][:, :].rearrange("p (k b) -> p k b", b=P),
                               ACT.Relu).then_inc(turn_hi[half], 1)

            act.wait_ge(bcol_ready, 1)
            for n in range(7):
                act.wait_ge(bot_full, n + 1)
                dst = bot0[:, n, :] if n < 4 else bot1[:, n - 4, :] if n < 6 else xT[:, :]
                act.activation(dst, sum_ps[n % 2][:, :], ACT.Relu, bias=bcol[:, n:n + 1]).then_inc(bot_read, 1)
            act.wait_ge(bot_read, 7)
            act.activation(xh[:, :], xT[:, :], ACT.Copy).then_inc(x_hi, 1)
            cut(W0)
            act.wait_ge(cleared, 3)
            act.activation(fh[:, :, 0], xT[:, 0:P], ACT.Copy).then_inc(feat_hi, 1)
            for g in range(NG):
                features(0, g)
                if 2 <= g < 6:
                    cut(W2A + g - 2)
            gram_out(0)
            for i in (W1, W3A, W3A + 1, W4):
                cut(i)
            pairs(0)
            with act.Fori(0, CHUNKS - 1) as c:
                bottom_feature(c + 1)
                features(c + 1, 0)
                features(c + 1, 1)
                relu_hi(h1h[:, 0:4, :], 0, 3 * c + 1)
                features(c + 1, 2)
                features(c + 1, 3)
                relu_hi(h1h[:, 4:8, :], 1, 2 * c + 1)
                features(c + 1, 4)
                features(c + 1, 5)
                relu_hi(h2h[:, 0:4, :], 0, 3 * c + 2)
                features(c + 1, 6)
                features(c + 1, 7)
                relu_hi(h2h[:, 4:8, :], 1, 2 * c + 2)
                gram_out(c + 1)
                relu_hi(h3h[:, :, :], 0, 3 * c + 3)
                pairs(c + 1)
            c = CHUNKS - 1
            relu_hi(h1h[:, 0:4, :], 0, 3 * c + 1)
            relu_hi(h1h[:, 4:8, :], 1, 2 * c + 1)
            relu_hi(h2h[:, 0:4, :], 0, 3 * c + 2)
            relu_hi(h2h[:, 4:8, :], 1, 2 * c + 2)
            relu_hi(h3h[:, :, :], 0, 3 * c + 3)
            act.wait_ge(logit_done, CHUNKS)
            act.activation(prob[:, :], logit[:, :], ACT.Sigmoid, bias=b5[:, 0:1]).then_inc(prob_done, 1)

        @block.vector
        def _(dve):
            def cut(i):
                dve.wait_ge(w_hi, i + 1)
                dve.tensor_tensor(piece[i][1], piece[i][2], piece[i][0].bitcast(F32), ALU.subtract).then_inc(w_lo, 1)

            def bottom_feature(c):
                dve.wait_ge(feat_hi, (NG + 1) * c + 1)
                dve.tensor_tensor(fl[:, :, 0], xT[:, bass.ds(c * P, P)], fh[:, :, 0].bitcast(F32),
                                  ALU.subtract).then_inc(feat_lo, 1)

            def features(c, g):
                n = GROUPS[g]
                dve.wait_ge(feat_hi, (NG + 1) * c + g + 2)
                cols = slice(1 + FIRST[g], 1 + FIRST[g] + n)
                dve.tensor_tensor(fl[:, :, cols], feat_ps[g % 2][:, 0:n * P].rearrange("p (f b) -> p b f", f=n),
                                  fh[:, :, cols].bitcast(F32), ALU.subtract).then_inc(feat_lo, 1)

            def gram_out(c):
                dve.wait_ge(gram_stored, 3 * DMA * c)
                for r in range(1, ZR, 2):
                    dve.wait_ge(gram_done, ZR * c + r + 1)
                    table = gram_ps[1][0:NF, 0:ZS * FS].rearrange("p (s j) -> p j s", s=ZS)
                    dve.tensor_copy(zs[0:NF, 0:JA, r * ZS:(r + 1) * ZS], table[:, 0:JA, :]).then_inc(gram_odd, 1)
                    dve.tensor_copy(zs[32:32 + NF, 0:NF - JA, r * ZS:(r + 1) * ZS],
                                    table[:, JA:NF, :]).then_inc(gram_odd, 1)

            def pairs(c):
                dve.wait_ge(pair_hi, c + 1)
                dve.tensor_tensor(rl[:, :, :], rraw[:, :, :], rh[:, :, :].bitcast(F32), ALU.subtract).then_inc(pair_lo, 1)

            def add_bias(half, count, width, bias):
                dve.wait_ge(sum_full[half], count)
                dve.tensor_tensor(sums[:, half * BANK:half * BANK + width], sum_ps[half][:, 0:width], bias,
                                  ALU.add).then_inc(sum_read[half], 1)

            def relu_lo(dst, hi, half, count):
                dve.wait_ge(turn_hi[half], count)
                dve.scalar_tensor_tensor(out=dst, in0=turn_ps[half][:, :].rearrange("p (k b) -> p k b", b=P),
                                         scalar=0.0, in1=hi.bitcast(F32), op0=ALU.max,
                                         op1=ALU.subtract).then_inc(turn_lo[half], 1)

            def last_layer(c):
                add_bias(1, 3 * c + 3, n4, b3[:, :])
                dve.wait_ge(sum_read[1], CHUNKS + 3 * c + 3)
                dve.scalar_tensor_tensor(out=sums[:, BANK + n4:BANK + 2 * n4], in0=sums[:, BANK:BANK + n4], scalar=0.0,
                                         in1=w5[:, :], op0=ALU.max, op1=ALU.mult,
                                         accum_out=dotc[:, :]).then_inc(dot_done, 1)
                dve.wait_ge(dot_done, c + 1)
                dve.tensor_copy(logit[:, bass.ds(c, 1)], dotc[:, :]).then_inc(logit_done, 1)

            steps = [0]

            def link(ins):
                steps[0] += 1
                ins.then_inc(chain, 1)
                dve.wait_ge(chain, steps[0])

            dve.wait_ge(idx_in, 2 * DMA)
            link(dve.tensor_scalar(idx_n[:, :], idx_i[:, :], 0.0, float(vocab), ALU.is_lt, ALU.mult))
            link(dve.tensor_tensor(idx_f[:, :], idx_n[:, :], idx_i[:, :], ALU.add))
            link(dve.tensor_scalar(idx_n[:, :], idx_f[:, :], 0.0, float(vocab - 1), ALU.max, ALU.min))
            link(dve.tensor_scalar(idx_f[:, :], idx_n[:, :], tbase[:, 0:1], None, ALU.add))
            dve.wait_ge(early_turned, 1)
            dve.tensor_copy(rows[:, :], turn_ps[0][:, 0:CHUNKS * n_tab]).then_inc(turn_lo[0], 1)
            dve.wait_ge(early_turned, 2)
            dve.tensor_copy(denT[:, :], turn_ps[1][0:n_dense, :]).then_inc(turn_lo[1], 1)
            dve.wait_ge(early_turned, 3)
            dve.tensor_copy(bcol[:, :], gram_ps[0][:, 0:7]).then_inc(bcol_ready, 1)
            dve.memset(fh[:, :, NF].bitcast(F32), 0.0).then_inc(cleared, 1)
            dve.memset(fl[:, :, NF].bitcast(F32), 0.0).then_inc(cleared, 1)
            dve.memset(rraw[:, :, :], 0.0).then_inc(cleared, 1)
            dve.wait_ge(x_hi, 1)
            dve.tensor_tensor(xl[:, :], xT[:, :], xh[:, :].bitcast(F32), ALU.subtract).then_inc(x_lo, 1)
            cut(W0)
            bottom_feature(0)
            dve.wait_ge(b0_in, DMA)

            def share(c):
                stage = (sums, xpart)[c % 2]
                if c >= 2:
                    dve.wait_ge(xp_stored[c % 2], DMA * (c // 2))
                for half in range(2):
                    dve.wait_ge(xp_full, 2 * c + half + 1)
                    dve.tensor_tensor(stage[:, half * BANK:(half + 1) * BANK], sum_ps[half][:, :],
                                      b0[:, half * BANK:(half + 1) * BANK], ALU.add).then_inc(sum_read[half], 1)

            features(0, 0)
            share(0)
            features(0, 1)
            share(1)
            features(0, 2)
            share(2)
            share(3)
            for g in range(3, NG):
                cut(W2A + g - 3) if g < 7 else None
                features(0, g)
            gram_out(0)
            for i in (W1, W3A, W3A + 1, W4):
                cut(i)
            pairs(0)
            dve.wait_ge(tail_in, 5 * DMA)
            with dve.Fori(0, CHUNKS - 1) as c:
                bottom_feature(c + 1)
                features(c + 1, 0)
                features(c + 1, 1)
                dve.wait_ge(xp_loaded, DMA * (c + 1))
                add_bias(0, 3 * c + 1, BANK, xpart[:, 0:BANK])
                relu_lo(h1l[:, 0:4, :], h1h[:, 0:4, :], 0, 3 * c + 1)
                add_bias(1, 3 * c + 1, BANK, xpart[:, BANK:2 * BANK])
                features(c + 1, 2)
                features(c + 1, 3)
                relu_lo(h1l[:, 4:8, :], h1h[:, 4:8, :], 1, 2 * c + 1)
                features(c + 1, 4)
                add_bias(0, 3 * c + 2, BANK, b1[:, 0:BANK])
                features(c + 1, 5)
                relu_lo(h2l[:, 0:4, :], h2h[:, 0:4, :], 0, 3 * c + 2)
                add_bias(1, 3 * c + 2, BANK, b1[:, BANK:2 * BANK])
                features(c + 1, 6)
                features(c + 1, 7)
                relu_lo(h2l[:, 4:8, :], h2h[:, 4:8, :], 1, 2 * c + 2)
                gram_out(c + 1)
                add_bias(0, 3 * c + 3, BANK, b2[:, :])
                relu_lo(h3l[:, :, :], h3h[:, :, :], 0, 3 * c + 3)
                pairs(c + 1)
                last_layer(c)
            c = CHUNKS - 1
            dve.wait_ge(xp_loaded, DMA * (c + 1))
            add_bias(0, 3 * c + 1, BANK, xpart[:, 0:BANK])
            relu_lo(h1l[:, 0:4, :], h1h[:, 0:4, :], 0, 3 * c + 1)
            add_bias(1, 3 * c + 1, BANK, xpart[:, BANK:2 * BANK])
            relu_lo(h1l[:, 4:8, :], h1h[:, 4:8, :], 1, 2 * c + 1)
            add_bias(0, 3 * c + 2, BANK, b1[:, 0:BANK])
            relu_lo(h2l[:, 0:4, :], h2h[:, 0:4, :], 0, 3 * c + 2)
            add_bias(1, 3 * c + 2, BANK, b1[:, BANK:2 * BANK])
            relu_lo(h2l[:, 4:8, :], h2h[:, 4:8, :], 1, 2 * c + 2)
            add_bias(0, 3 * c + 3, BANK, b2[:, :])
            relu_lo(h3l[:, :, :], h3h[:, :, :], 0, 3 * c + 3)
            last_layer(c)

        @block.tensor
        def _(pe):
            def product(dst, left, right, first, last):
                pe.matmul(dst, left[0], right[0], start=first, stop=False)
                pe.matmul(dst, left[0], right[1], start=False, stop=False)
                return pe.matmul(dst, left[1], right[0], start=False, stop=last)

            def features(c, g):
                s = g % SLOTS
                n = GROUPS[g]
                pe.wait_ge(slot_loaded[s], DMA * n * (NG // SLOTS * c + g // SLOTS + 1))
                if not (isinstance(c, int) and c == 0 and g < 2):
                    pe.wait_ge(feat_lo, (NG + 1) * c + g)
                for k in range(n):
                    t = pe.transpose(feat_ps[g % 2][:, k * P:(k + 1) * P], gat[:, SLOT0[s] + k, :], ident[:, :])
                t.then_inc(turned, 1)

            def gram(c):
                pe.wait_ge(feat_lo, (NG + 1) * (c + 1))
                for r in range(ZR):
                    if r % 2 == 0:
                        pe.wait_ge(gram_even, 2 * (ZR // 2 * c + r // 2))
                    else:
                        pe.wait_ge(gram_odd, 2 * (ZR // 2 * c + r // 2))
                    for s in range(ZS):
                        b = r * ZS + s
                        m = product(gram_ps[r % 2][0:NF, s * FS:(s + 1) * FS], (fh[:, b, 0:NF], fl[:, b, 0:NF]),
                                    (fh[:, b, :], fl[:, b, :]), True, True)
                    m.then_inc(gram_done, 1)

            def first_layer(half, tiles):
                cols = slice(half * BANK, (half + 1) * BANK)
                for t in tiles:
                    m = product(sum_ps[half][:, :], (rh[:, t, :], rl[:, t, :]), (w1h[:, t, cols], w1l[:, t, cols]),
                                t == 0, t == 2)
                if t == 2:
                    m.then_inc(sum_full[half], 1)

            def second_layer(half, tiles):
                cols = slice(half * BANK, (half + 1) * BANK)
                for k in tiles:
                    m = product(sum_ps[half][:, :], (h1h[:, k, :], h1l[:, k, :]), (w2h[:, k, cols], w2l[:, k, cols]),
                                k == 0, k == K1 - 1)
                if k == K1 - 1:
                    m.then_inc(sum_full[half], 1)

            def turn(half, summed, copied):
                pe.wait_ge(sum_read[half], CHUNKS + summed)
                pe.wait_ge(turn_lo[half], 1 + copied)
                for k in range(4):
                    at_ = half * BANK + k * P
                    t = pe.transpose(turn_ps[half][:, k * P:(k + 1) * P], sums[:, at_:at_ + P], ident[:, :])
                t.then_inc(turn_full[half], 1)

            def mlp_front(c, nxt):
                if nxt is not None:
                    features(nxt, 0)
                    features(nxt, 1)
                pe.wait_ge(pair_lo, c + 1)
                pe.wait_ge(sum_read[0], CHUNKS + 3 * c)
                first_layer(0, range(3))
                pe.wait_ge(sum_read[1], CHUNKS + 3 * c)
                first_layer(1, range(2))
                turn(0, 3 * c + 1, 3 * c)
                first_layer(1, range(2, 3))
                if nxt is not None:
                    features(nxt, 2)
                    features(nxt, 3)
                pe.wait_ge(turn_lo[0], 3 * c + 2)
                second_layer(0, range(4))
                turn(1, 3 * c + 1, 2 * c)
                second_layer(1, range(4))
                if nxt is not None:
                    features(nxt, 4)
                pe.wait_ge(turn_lo[1], 2 * c + 2)
                second_layer(0, range(4, 8))
                if nxt is not None:
                    features(nxt, 5)
                second_layer(1, range(4, 6))
                turn(0, 3 * c + 2, 3 * c + 1)
                second_layer(1, range(6, 8))
                if nxt is not None:
                    features(nxt, 6)
                    features(nxt, 7)
                turn(1, 3 * c + 2, 2 * c + 1)

            def mlp_back(c):
                pe.wait_ge(turn_lo[0], 3 * c + 3)
                for k in range(K2):
                    if k == 4:
                        pe.wait_ge(turn_lo[1], 2 * c + 3)
                    m = product(sum_ps[0][:, :], (h2h[:, k, :], h2l[:, k, :]), (w3h[:, k, :], w3l[:, k, :]),
                                k == 0, k == K2 - 1)
                m.then_inc(sum_full[0], 1)
                turn(0, 3 * c + 3, 3 * c + 2)
                pe.wait_ge(turn_lo[0], 3 * c + 4)
                pe.wait_ge(sum_read[1], CHUNKS + 3 * c + 2)
                for k in range(K3):
                    m = product(sum_ps[1][:, 0:n4], (h3h[:, k, :], h3l[:, k, :]), (w4h[:, k, :], w4l[:, k, :]),
                                k == 0, k == K3 - 1)
                m.then_inc(sum_full[1], 1)

            pe.wait_ge(ident_ready, 1)
            pe.wait_ge(chain, 4)
            by_chunk = idx_f[:, :].rearrange("f (p c) -> f c p", c=CHUNKS)
            for c in range(CHUNKS):
                t = pe.transpose(turn_ps[0][:, c * n_tab:(c + 1) * n_tab], by_chunk[:, c, :], ident[0:n_tab, 0:n_tab])
            t.then_inc(early_turned, 1)
            pe.wait_ge(den_in, DMA)
            for c in range(CHUNKS):
                t = pe.transpose(turn_ps[1][0:n_dense, c * P:(c + 1) * P], den[:, c * n_dense:(c + 1) * n_dense],
                                 ident[:, :])
            t.then_inc(early_turned, 1)
            pe.wait_ge(bias_in, 3 * DMA)
            pe.transpose(gram_ps[0][:, 0:7], brow[:, :], ident[0:7, 0:7]).then_inc(early_turned, 1)
            pe.wait_ge(turn_lo[1], 1)
            pe.wait_ge(bot_w_in, 3 * DMA)
            for n in range(7):
                if n >= 2:
                    pe.wait_ge(bot_read, n - 1)
                if n < 4:
                    m = pe.matmul(sum_ps[n % 2][:, :], bw0s[:, n * P:(n + 1) * P], denT[:, :], start=True, stop=True)
                elif n < 6:
                    pe.wait_ge(bot_read, 4)
                    for k in range(4):
                        m = pe.matmul(sum_ps[n % 2][:, :], bw1s[:, k, (n - 4) * P:(n - 3) * P], bot0[:, k, :],
                                      start=k == 0, stop=k == 3)
                else:
                    pe.wait_ge(bot_read, 6)
                    for k in range(2):
                        m = pe.matmul(sum_ps[n % 2][:, :], bw2s[:, k, :], bot1[:, k, :], start=k == 0, stop=k == 1)
                m.then_inc(bot_full, 1)
            features(0, 0)
            pe.wait_ge(bot_read, 7)
            pe.wait_ge(x_lo, 1)
            pe.wait_ge(w_lo, W0 + 1)
            for c in range(CHUNKS):
                for half in range(2):
                    if c >= 1:
                        pe.wait_ge(sum_read[half], c)
                    cols = slice(half * BANK, (half + 1) * BANK)
                    product(sum_ps[half][:, :], (xh[:, c * P:(c + 1) * P], xl[:, c * P:(c + 1) * P]),
                            (w0h[:, cols], w0l[:, cols]), True, True).then_inc(xp_full, 1)
                if c < 2:
                    features(0, c + 1)
            for g in range(3, NG):
                features(0, g)
            gram(0)
            pe.wait_ge(w_lo, W4 + 1)
            with pe.Fori(0, CHUNKS - 1) as c:
                mlp_front(c, c + 1)
                gram(c + 1)
                mlp_back(c)
            mlp_front(CHUNKS - 1, None)
            mlp_back(CHUNKS - 1)


_INS = ["r_dense", "r_indices"] + ["L0_rec_" + n for n in (
    "emb_tables", "bw0", "bb0", "bw1", "bb1", "bw2", "bb2", "tw0", "tb0", "tw1", "tb1", "tw2", "tb2",
    "tw3", "tb3", "tw4", "tb4")]


def kernel(**inputs):
    import numpy as np
    import concourse.bacc as bacc
    from concourse.bass_utils import run_bass_kernel_spmd

    nc = bacc.Bacc("TRN2", target_bir_lowering=False, num_devices=1)
    arrays, args = {}, []

    def give(name, a):
        arrays[name] = a
        args.append(nc.dram_tensor(name, a.shape, mybir.dt.from_np(a.dtype), kind="ExternalInput").ap())

    for name in _INS:
        give(f"in_{name}", np.ascontiguousarray(inputs[name]))
    n_tab, vocab, emb = inputs["L0_rec_emb_tables"].shape
    give("pair_row", np.array(pair_rows(n_tab + 1, emb), np.uint32))
    give("table_base", (np.arange(n_tab, dtype=np.float32) * vocab).reshape(n_tab, 1))
    batch = inputs["r_dense"].shape[0]
    args.append(nc.dram_tensor("out_0", (batch, 1), F32, kind="ExternalOutput").ap())
    dlrm_program(nc, *args)
    r = run_bass_kernel_spmd(nc, [arrays], core_ids=[0])
    return r.results[0]["out_0"]
```

```python
from contextlib import ExitStack

import concourse.bass as bass
from concourse import mybir

ALU = mybir.AluOpType
ACT = mybir.ActivationFunctionType
F32 = mybir.dt.float32
F32R = mybir.dt.float32r
I32 = mybir.dt.int32
U32 = mybir.dt.uint32

P = 128
BANK = 512
GROUPS = (4, 3, 3, 3) * 2
DMA = 16


def pair_rows(n_feat, first_row):
    def row(i, j):
        a, b = min(i, j % n_feat), max(i, j % n_feat)
        return first_row + a * n_feat - a * (a + 1) // 2 + b - a - 1

    near = [[row(i, i + 1 + 3 * q + t) for t in range(3)] for i in range(n_feat) for q in range(4)]
    far = [[row(n_feat // 3 * t + r, n_feat // 3 * t + r + 13) for t in range(3)] for r in range(n_feat // 3)]
    return near + far


def dlrm_program(nc, dense, indices, tables, bw0, bb0, bw1, bb1, bw2, bb2,
                 tw0, tb0, tw1, tb1, tw2, tb2, tw3, tb3, tw4, tb4, pair_row, table_base, out):
    B, n_dense = dense.shape
    n_tab, vocab, emb = tables.shape
    CHUNKS = B // P
    NF = n_tab + 1
    n1, n2, n3, n4 = tw0.shape[1], tw1.shape[1], tw2.shape[1], tw3.shape[1]
    U0, U1 = bw0.shape[1], bw1.shape[1]
    K1, K2, K3 = n1 // P, n2 // P, n3 // P
    NG = len(GROUPS)
    FIRST = [sum(GROUPS[:g]) for g in range(NG)]
    ZS = 16
    ZR = P // ZS
    JA = 14
    PK = NF * (NF - 1) // 2 // 3
    JW = NF + 13
    assert (emb, NF, n1, n2, n3, n4) == (P, 27, 1024, 1024, 512, 256) and sum(GROUPS) == n_tab

    with ExitStack() as ctx:
        def sem(name):
            return ctx.enter_context(nc.semaphore(name))

        place = [(nc.sbuf_base + 31) // 32 * 32]

        def at(name, shape, dt, offset):
            return nc.alloc_sbuf_tensor_at(name, shape, dt, offset=offset)

        def new(name, shape, dt=F32):
            size = 4
            for n in shape[1:]:
                size *= n
            offset = place[0]
            place[0] += (size + 31) // 32 * 32
            return at(name, shape, dt, offset), offset

        def parts(name, shape):
            hi, hi_at = new(name + "_hi", shape, F32R)
            lo, lo_at = new(name + "_lo", shape, F32R)
            return hi, lo, at(name + "_raw", shape, F32, lo_at), hi_at, lo_at

        w1h, w1l, w1raw, _, _ = parts("w1", [PK, 3, n1])
        w2h, w2l, w2raw, _, _ = parts("w2", [P, K1, n2])
        w3h, w3l, w3raw, w3_at, _ = parts("w3", [P, K2, n3])
        w4h, w4l, w4raw, _, _ = parts("w4", [P, K3, n4])
        feat, _ = new("feat", [P, P, NF])
        rh, _ = new("pair_hi", [PK, 3, P], F32R)
        rl, _ = new("pair_lo", [PK, 3, P], F32R)
        rraw = rl[:, :, :].bitcast(F32)
        h1h, h1_at = new("h1_hi", [P, K1, P], F32R)
        h1l, h1l_at = new("h1_lo", [P, K1, P], F32R)
        h2h, _ = new("h2_hi", [P, K2, P], F32R)
        h2l, _ = new("h2_lo", [P, K2, P], F32R)
        h3h, _ = new("h3_hi", [P, K3, P], F32R)
        h3l, _ = new("h3_lo", [P, K3, P], F32R)
        gat, _ = new("gathered", [P, n_tab, emb])
        zs, zs_at = new("gram", [P, JA, P])
        xpart, _ = new("xpart", [P, n1])
        sums, _ = new("sums", [P, n1])
        sums3, _ = new("sums3", [P, n3])
        b1, _ = new("b1", [P, n2])
        b2, _ = new("b2", [P, n3])
        b3, _ = new("b3", [P, n4])
        w5, _ = new("w5", [P, n4])
        b5, _ = new("b5", [P, 1])
        xT, _ = new("xT", [P, B])
        ident, _ = new("ident", [P, P])
        rows, _ = new("rows", [P, CHUNKS * n_tab], U32)
        prow, _ = new("prow", [PK, 3], U32)
        tbase, _ = new("tbase", [n_tab, 1])
        dotc, _ = new("dotc", [P, 1])
        logit, _ = new("logit", [P, CHUNKS])
        prob, _ = new("prob", [P, CHUNKS])
        assert place[0] <= nc.sbuf_usable_end, place[0] - nc.sbuf_usable_end
        w0h = at("w0_hi", [P, n1], F32R, h1_at)
        w0l = at("w0_lo", [P, n1], F32R, h1l_at)
        w0raw = at("w0_raw", [P, n1], F32, h1l_at)
        idx_i = at("idx_i", [n_tab, B], I32, zs_at)
        idx_n = at("idx_n", [n_tab, B], F32, zs_at + 4 * B)
        idx_f = at("idx_f", [n_tab, B], F32, zs_at + 8 * B)
        early = [w3_at]

        def new_early(name, shape, dt=F32):
            size = 4
            for n in shape[1:]:
                size *= n
            early[0] += (size + 31) // 32 * 32
            return at(name, shape, dt, early[0] - (size + 31) // 32 * 32)

        bot0 = new_early("bot0", [P, U0 // P, B])
        bot1 = new_early("bot1", [P, U1 // P, B])
        bw0s = new_early("bw0s", [n_dense, U0])
        bw1s = new_early("bw1s", [P, U0 // P, U1])
        bw2s = new_early("bw2s", [P, U1 // P, emb])
        den = new_early("den", [P, CHUNKS * n_dense])
        denT = new_early("denT", [n_dense, B])
        brow = new_early("brow", [7, P])
        bcol = new_early("bcol", [P, 7])
        b0 = new_early("b0", [P, n1])
        xh = new_early("x_hi", [P, B], F32R)
        xl = new_early("x_lo", [P, B], F32R)
        assert early[0] <= w3_at + 2 * 4 * K2 * n3

        feat_ps = [ctx.enter_context(nc.psum_tensor(f"feat_ps{i}", [P, BANK], F32)) for i in range(2)]
        gram_ps = [ctx.enter_context(nc.psum_tensor(f"gram_ps{i}", [P, BANK], F32)) for i in range(2)]
        sum_ps = [ctx.enter_context(nc.psum_tensor(f"sum_ps{i}", [P, BANK], F32)) for i in range(2)]
        turn_ps = [ctx.enter_context(nc.psum_tensor(f"turn_ps{i}", [P, BANK], F32)) for i in range(2)]

        early_ps = [sum_ps[0], sum_ps[1], gram_ps[0], gram_ps[1]]

        GRAM = NF * (JW + 1) * P
        gram_dram = nc.dram_tensor("gram_dram", (CHUNKS * GRAM,), F32, kind="Internal").ap()
        xpart_dram = nc.dram_tensor("xpart_dram", (CHUNKS * P * n1,), F32, kind="Internal").ap()

        idx_in, den_in, bias_in = sem("idx_in"), sem("den_in"), sem("bias_in")
        bw0_in, bot_w_in = sem("bw0_in"), sem("bot_w_in")
        prow_in, b0_in, tail_in = sem("prow_in"), sem("b0_in"), sem("tail_in")
        w_in = [sem(f"w_in{i}") for i in range(9)]
        w_hi, w_lo = sem("w_hi"), sem("w_lo")
        ident_step, ident_ready = sem("ident_step"), sem("ident_ready")
        chain = sem("vector_chain")
        early_turned, bcol_ready = sem("early_turned"), sem("bcol_ready")
        bot_full = sem("bot_full")
        bot_act, bot_dve = sem("bot_read_scalar"), sem("bot_read_vector")
        x_hi, x_raw, x_lo = sem("x_hi_ready"), sem("x_ready"), sem("x_lo_ready")
        xp_full = sem("xp_full")
        xp_stored = [sem(f"xp_stored{i}") for i in range(2)]
        xp_loaded = sem("xp_loaded")
        loaded = [sem(f"group_loaded{g}") for g in range(NG)]
        turned = sem("features_turned")
        feat_x, feat_even, feat_odd = sem("feat_x"), sem("feat_even"), sem("feat_odd")
        gram_done = sem("gram_done")
        gram_even, gram_odd = sem("gram_even"), sem("gram_odd")
        gram_stored, pair_loaded = sem("gram_stored"), sem("pair_loaded")
        pair_hi, pair_lo = sem("pair_hi_ready"), sem("pair_lo_ready")
        sum_full = [sem(f"sum_full{i}") for i in range(2)]
        third_full, fourth_full = sem("third_full"), sem("fourth_full")
        sum_read = [sem(f"sum_read{i}") for i in range(2)]
        third_read, fourth_read = sem("third_read"), sem("fourth_read")
        turn_full = [sem(f"turn_full{i}") for i in range(2)]
        turn_hi = [sem(f"turn_hi{i}") for i in range(2)]
        turn_lo = [sem(f"turn_lo{i}") for i in range(2)]
        dot_done, logit_done, prob_done, out_done = (
            sem("dot_done"), sem("logit_done"), sem("prob_done"), sem("out_done"))

        W0, W1, W2A, W3A, W4 = 0, 1, 2, 6, 8
        piece = [(w0h[:, :], w0l[:, :], w0raw[:, :])]
        piece += [(w1h[:, :, :], w1l[:, :, :], w1raw[:, :, :])]
        piece += [(w2h[:, 2 * i:2 * i + 2, :], w2l[:, 2 * i:2 * i + 2, :], w2raw[:, 2 * i:2 * i + 2, :]) for i in range(4)]
        piece += [(w3h[:, 4 * i:4 * i + 4, :], w3l[:, 4 * i:4 * i + 4, :], w3raw[:, 4 * i:4 * i + 4, :]) for i in range(2)]
        piece += [(w4h[:, :, :], w4l[:, :, :], w4raw[:, :, :])]

        block = ctx.enter_context(nc.Block())

        @block.gpsimd
        def _(pool):
            pool.memset(ident[:, :], 0.0).then_inc(ident_step, 1)
            pool.wait_ge(ident_step, 1)
            pool.affine_select(out=ident[:, :], in_=ident[:, :], compare_op=ALU.not_equal, fill=1.0,
                               base=0, pattern=[[-1, P]], channel_multiplier=1).then_inc(ident_ready, 1)
            pool.wait_ge(prow_in, DMA)
            for t in range(3):
                pool.indirect_dma_start(
                    out=w1raw[:, t, :], out_offset=None, in_=tw0,
                    in_offset=bass.IndirectOffsetOnAxis(ap=prow[:, t:t + 1], axis=0),
                ).then_inc(w_in[W1], DMA)
            pool.wait_ge(turn_lo[0], 1)
            all_rows = tables.rearrange("t v e -> (t v) e")
            for c in range(CHUNKS):
                for g, size in enumerate(GROUPS):
                    if c > 0:
                        pool.wait_ge(turned, NG * (c - 1) + g + 1)
                    for k in range(FIRST[g], FIRST[g] + size):
                        col = c * n_tab + k
                        pool.indirect_dma_start(
                            out=gat[:, k, :], out_offset=None, in_=all_rows,
                            in_offset=bass.IndirectOffsetOnAxis(ap=rows[:, col:col + 1], axis=0),
                        ).then_inc(loaded[g], DMA)

        @block.sync
        def _(sp):
            sp.dma_start(idx_i[:, :], indices).then_inc(idx_in, DMA)
            sp.dma_start(tbase[:, :], table_base).then_inc(idx_in, DMA)
            sp.dma_start(prow[:, :], pair_row).then_inc(prow_in, DMA)
            sp.dma_start(den[:, :], dense.rearrange("(p c) k -> p (c k)", c=CHUNKS)).then_inc(den_in, DMA)
            sp.dma_start(bw0s[:, :], bw0).then_inc(bw0_in, DMA)
            sp.dma_start(brow[0:4, :], bb0.rearrange("(m p) -> m p", p=P)).then_inc(bias_in, DMA)
            sp.dma_start(brow[4:6, :], bb1.rearrange("(m p) -> m p", p=P)).then_inc(bias_in, DMA)
            sp.dma_start(brow[6:7, :], bb2.rearrange("(m p) -> m p", p=P)).then_inc(bias_in, DMA)
            sp.dma_start(bw1s[:, :, :], bw1.rearrange("(k p) n -> p k n", p=P)).then_inc(bot_w_in, DMA)
            sp.dma_start(bw2s[:, :, :], bw2.rearrange("(k p) n -> p k n", p=P)).then_inc(bot_w_in, DMA)
            sp.dma_start(w0raw[:, :], tw0[0:P, :]).then_inc(w_in[W0], DMA)
            sp.dma_start(b0[:, :], tb0.partition_broadcast(P)).then_inc(b0_in, DMA)
            w2_rows = tw1.rearrange("(k p) n -> p k n", p=P)
            for i in range(4):
                sp.wait_ge(loaded[i], DMA * GROUPS[i])
                sp.dma_start(w2raw[:, 2 * i:2 * i + 2, :], w2_rows[:, 2 * i:2 * i + 2, :]).then_inc(w_in[W2A + i], DMA)
            sp.wait_ge(loaded[4], DMA * GROUPS[4])
            sp.dma_start(b1[:, :], tb1.partition_broadcast(P)).then_inc(tail_in, DMA)
            sp.dma_start(b2[:, :], tb2.partition_broadcast(P)).then_inc(tail_in, DMA)
            sp.dma_start(b3[:, :], tb3.partition_broadcast(P)).then_inc(tail_in, DMA)
            sp.dma_start(w5[:, :], tw4.rearrange("n o -> (n o)").partition_broadcast(P)).then_inc(tail_in, DMA)
            sp.dma_start(b5[:, :], tb4.partition_broadcast(P)).then_inc(tail_in, DMA)
            w4_rows = tw3.rearrange("(k p) n -> p k n", p=P)
            for c in range(CHUNKS):
                sp.wait_ge(sum_read[0], c + 1)
                sp.wait_ge(sum_read[1], c + 1)
                stage = (sums, xpart)[c % 2]
                sp.dma_start(xpart_dram[c * P * n1:(c + 1) * P * n1].rearrange("(p n) -> p n", p=P), stage[:, :]).then_inc(xp_stored[c % 2], DMA)
            w3_rows = tw2.rearrange("(k p) n -> p k n", p=P)
            for i in range(2):
                sp.dma_start(w3raw[:, 4 * i:4 * i + 4, :], w3_rows[:, 4 * i:4 * i + 4, :]).then_inc(w_in[W3A + i], DMA)
            sp.dma_start(w4raw[:, :, :], w4_rows).then_inc(w_in[W4], DMA)
            sp.wait_ge(xp_stored[0], DMA * (CHUNKS // 2))
            sp.wait_ge(xp_stored[1], DMA * (CHUNKS // 2))
            sp.dma_start(xpart[:, :], xpart_dram[0:P * n1].rearrange("(p n) -> p n", p=P)).then_inc(xp_loaded, DMA)

            def pairs_through_dram(start, copied, stored):
                flat = gram_dram[bass.ds(start, GRAM)]
                by_row = flat[0:NF * JW * P].rearrange("(i j b) -> i j b", i=NF, j=JW)
                skewed = flat.rearrange("(i j b) -> i j b", i=NF, j=JW + 1)
                sp.wait_ge(gram_even, copied)
                sp.wait_ge(gram_odd, copied)
                sp.dma_start(by_row[:, JA:NF, :], zs[32:32 + NF, 0:NF - JA, :]).then_inc(gram_stored, DMA)
                sp.dma_start(by_row[0:13, 1:JA, :], zs[0:13, 1:JA, :]).then_inc(gram_stored, DMA)
                sp.dma_start(by_row[14:NF, NF:JW, :], zs[14:NF, 0:13, :]).then_inc(gram_stored, DMA)
                sp.wait_ge(gram_stored, stored)
                sp.dma_start(rraw[0:4 * NF, :, :].rearrange("p t b -> p (t b)"),
                             skewed[:, 1:13, :].rearrange("i (q t) b -> i q (t b)", q=4)).then_inc(pair_loaded, DMA)
                sp.dma_start(rraw[4 * NF:PK, :, :],
                             skewed[:, 13, :].rearrange("(t r) b -> r t b", t=3)).then_inc(pair_loaded, DMA)

            pairs_through_dram(0, ZR, 3 * DMA)
            with sp.Fori(0, CHUNKS - 1) as c:
                shared = sp.snap(2 * c + CHUNKS + 1)
                copied = sp.snap(ZR * c + 2 * ZR)
                stored = sp.snap(3 * DMA * c + 6 * DMA)
                xpart_at = sp.snap((c + 1) * (P * n1))
                gram_at = sp.snap((c + 1) * GRAM)
                sp.wait_ge(sum_read[0], shared)
                sp.wait_ge(sum_read[1], shared)
                sp.dma_start(xpart[:, :], xpart_dram[bass.ds(xpart_at, P * n1)].rearrange("(p n) -> p n", p=P)).then_inc(xp_loaded, DMA)
                pairs_through_dram(gram_at, copied, stored)
            sp.wait_ge(prob_done, 2)
            sp.dma_start(out.rearrange("(p c) o -> p (c o)", c=CHUNKS), prob[:, :]).then_inc(out_done, DMA)
            sp.wait_ge(out_done, DMA)

        @block.scalar
        def _(act):
            def cut(i):
                act.wait_ge(w_in[i], 3 * DMA if i == W1 else DMA)
                act.activation(piece[i][0], piece[i][2], ACT.Copy).then_inc(w_hi, 1)

            def bottom_feature(c):
                act.wait_ge(gram_done, ZR * c)
                act.activation(feat[:, :, 0], xT[:, bass.ds(c * P, P)], ACT.Copy).then_inc(feat_x, 1)

            def features(c, g):
                n = GROUPS[g]
                act.wait_ge(turned, NG * c + g + 1)
                act.activation(feat[:, :, 1 + FIRST[g]:1 + FIRST[g] + n],
                               feat_ps[0][:, 0:n * P].rearrange("p (f b) -> p b f", f=n),
                               ACT.Copy).then_inc(feat_even, 1)

            def gram_out(c):
                act.wait_ge(gram_stored, 3 * DMA * c)
                for r in range(0, ZR, 2):
                    act.wait_ge(gram_done, ZR * c + r + 1)
                    table = gram_ps[0][0:NF, 0:ZS * NF].rearrange("p (s j) -> p j s", s=ZS)
                    act.activation(zs[0:NF, 0:JA, r * ZS:(r + 1) * ZS], table[:, 0:JA, :],
                                   ACT.Copy).then_inc(gram_even, 1)
                    act.activation(zs[32:32 + NF, 0:NF - JA, r * ZS:(r + 1) * ZS], table[:, JA:NF, :],
                                   ACT.Copy).then_inc(gram_even, 1)

            def pairs(c):
                act.wait_ge(pair_loaded, 2 * DMA * (c + 1))
                act.activation(rh[:, :, :], rraw[:, :, :], ACT.Copy).then_inc(pair_hi, 1)

            def relu_hi(dst, half, count):
                act.wait_ge(turn_full[half], count)
                act.activation(dst, turn_ps[half][:, :].rearrange("p (k b) -> p k b", b=P),
                               ACT.Relu).then_inc(turn_hi[half], 1)

            def bottom_relu(n, dst):
                act.wait_ge(bot_full, n + 1)
                act.activation(dst, early_ps[n % 4][:, :], ACT.Relu, bias=bcol[:, n:n + 1]).then_inc(bot_act, 1)

            act.wait_ge(early_turned, 3)
            act.activation(bcol[:, :], feat_ps[0][:, 0:7], ACT.Copy).then_inc(bcol_ready, 1)
            act.wait_ge(bcol_ready, 1)
            bottom_relu(0, bot0[:, 0, :])
            bottom_relu(2, bot0[:, 2, :])
            cut(W0)
            cut(W1)
            bottom_relu(4, bot1[:, 0, :])
            features(0, 0)
            cut(W2A)
            act.wait_ge(bot_full, 7)
            act.activation(xh[:, :], early_ps[2][:, :], ACT.Relu, bias=bcol[:, 6:7]).then_inc(x_hi, 1)
            features(0, 2)
            act.wait_ge(x_raw, 1)
            act.activation(feat[:, :, 0], xT[:, 0:P], ACT.Copy).then_inc(feat_x, 1)
            cut(W2A + 1)
            features(0, 4)
            cut(W2A + 2)
            cut(W2A + 3)
            features(0, 6)
            gram_out(0)
            cut(W3A)
            cut(W3A + 1)
            pairs(0)
            relu_hi(h1h[:, 0:4, :], 0, 1)
            relu_hi(h1h[:, 4:8, :], 1, 1)
            cut(W4)

            def second_out(c):
                relu_hi(h2h[:, 0:4, :], 0, 2 * c + 2)
                relu_hi(h2h[:, 4:8, :], 1, 3 * c + 2)

            with act.Fori(0, CHUNKS - 1) as c:
                bottom_feature(c + 1)
                for g in range(0, NG, 2):
                    features(c + 1, g)
                gram_out(c + 1)
                second_out(c)
                pairs(c + 1)
                relu_hi(h3h[:, :, :], 1, 3 * c + 3)
                relu_hi(h1h[:, 0:4, :], 0, 2 * c + 3)
                relu_hi(h1h[:, 4:8, :], 1, 3 * c + 4)
            second_out(CHUNKS - 1)
            relu_hi(h3h[:, :, :], 1, 3 * CHUNKS)
            for cols, chunks in ((slice(0, CHUNKS - 1), CHUNKS - 1), (slice(CHUNKS - 1, CHUNKS), CHUNKS)):
                act.wait_ge(logit_done, chunks)
                act.activation(prob[:, cols], logit[:, cols], ACT.Sigmoid, bias=b5[:, 0:1]).then_inc(prob_done, 1)

        @block.vector
        def _(dve):
            def cut(i):
                dve.wait_ge(w_hi, i + 1)
                dve.tensor_tensor(piece[i][1], piece[i][2], piece[i][0].bitcast(F32), ALU.subtract).then_inc(w_lo, 1)

            def features(c, g):
                n = GROUPS[g]
                dve.wait_ge(turned, NG * c + g + 1)
                dve.tensor_copy(feat[:, :, 1 + FIRST[g]:1 + FIRST[g] + n],
                                feat_ps[1][:, 0:n * P].rearrange("p (f b) -> p b f", f=n)).then_inc(feat_odd, 1)

            def gram_out(c):
                dve.wait_ge(gram_stored, 3 * DMA * c)
                for r in range(1, ZR, 2):
                    dve.wait_ge(gram_done, ZR * c + r + 1)
                    table = gram_ps[1][0:NF, 0:ZS * NF].rearrange("p (s j) -> p j s", s=ZS)
                    dve.tensor_copy(zs[0:NF, 0:JA, r * ZS:(r + 1) * ZS], table[:, 0:JA, :]).then_inc(gram_odd, 1)
                    dve.tensor_copy(zs[32:32 + NF, 0:NF - JA, r * ZS:(r + 1) * ZS],
                                    table[:, JA:NF, :]).then_inc(gram_odd, 1)

            def pairs(c):
                dve.wait_ge(pair_hi, c + 1)
                dve.tensor_tensor(rl[:, :, :], rraw[:, :, :], rh[:, :, :].bitcast(F32), ALU.subtract).then_inc(pair_lo, 1)

            def add_bias(half, count, bias):
                dve.wait_ge(sum_full[half], count)
                dve.tensor_tensor(sums[:, half * BANK:(half + 1) * BANK], sum_ps[half][:, :], bias,
                                  ALU.add).then_inc(sum_read[half], 1)

            def relu_lo(dst, hi, half, count):
                dve.wait_ge(turn_hi[half], count)
                dve.scalar_tensor_tensor(out=dst, in0=turn_ps[half][:, :].rearrange("p (k b) -> p k b", b=P),
                                         scalar=0.0, in1=hi.bitcast(F32), op0=ALU.max,
                                         op1=ALU.subtract).then_inc(turn_lo[half], 1)

            def third_sums(c):
                dve.wait_ge(third_full, c + 1)
                dve.tensor_tensor(sums3[:, :], gram_ps[0][:, :], b2[:, :], ALU.add).then_inc(third_read, 1)

            def last_layer(c):
                dve.wait_ge(fourth_full, c + 1)
                dve.tensor_tensor(sums3[:, 0:n4], gram_ps[1][:, 0:n4], b3[:, :], ALU.add).then_inc(fourth_read, 1)
                dve.wait_ge(fourth_read, c + 1)
                dve.scalar_tensor_tensor(out=sums3[:, n4:2 * n4], in0=sums3[:, 0:n4], scalar=0.0,
                                         in1=w5[:, :], op0=ALU.max, op1=ALU.mult,
                                         accum_out=dotc[:, :]).then_inc(dot_done, 1)
                dve.wait_ge(dot_done, c + 1)
                dve.tensor_copy(logit[:, bass.ds(c, 1)], dotc[:, :]).then_inc(logit_done, 1)

            steps = [0]

            def link(ins):
                steps[0] += 1
                ins.then_inc(chain, 1)
                dve.wait_ge(chain, steps[0])

            dve.wait_ge(idx_in, 2 * DMA)
            link(dve.tensor_scalar(idx_n[:, :], idx_i[:, :], 0.0, float(vocab), ALU.is_lt, ALU.mult))
            link(dve.tensor_tensor(idx_f[:, :], idx_n[:, :], idx_i[:, :], ALU.add))
            link(dve.tensor_scalar(idx_n[:, :], idx_f[:, :], 0.0, float(vocab - 1), ALU.max, ALU.min))
            link(dve.tensor_scalar(idx_f[:, :], idx_n[:, :], tbase[:, 0:1], None, ALU.add))
            dve.wait_ge(early_turned, 1)
            dve.tensor_copy(rows[:, :], turn_ps[0][:, 0:CHUNKS * n_tab]).then_inc(turn_lo[0], 1)
            dve.wait_ge(early_turned, 2)
            dve.tensor_copy(denT[:, :], turn_ps[1][0:n_dense, :]).then_inc(turn_lo[1], 1)
            dve.wait_ge(bcol_ready, 1)

            def bottom_relu(n, dst):
                dve.wait_ge(bot_full, n + 1)
                return dve.tensor_scalar(dst, early_ps[n % 4][:, :], bcol[:, n:n + 1], 0.0, ALU.add, ALU.max)

            bottom_relu(1, bot0[:, 1, :]).then_inc(bot_dve, 1)
            bottom_relu(3, bot0[:, 3, :]).then_inc(bot_dve, 1)
            cut(W0)
            cut(W1)
            bottom_relu(5, bot1[:, 1, :]).then_inc(bot_dve, 1)
            features(0, 1)
            cut(W2A)
            dve.wait_ge(x_hi, 1)
            bottom_relu(6, xT[:, :]).then_inc(x_raw, 1)
            dve.wait_ge(x_raw, 1)
            dve.tensor_tensor(xl[:, :], xT[:, :], xh[:, :].bitcast(F32), ALU.subtract).then_inc(x_lo, 1)
            dve.wait_ge(b0_in, DMA)

            def share(c):
                stage = (sums, xpart)[c % 2]
                if c >= 2:
                    dve.wait_ge(xp_stored[c % 2], DMA * (c // 2))
                for half in range(2):
                    dve.wait_ge(xp_full, 2 * c + half + 1)
                    dve.tensor_tensor(stage[:, half * BANK:(half + 1) * BANK], early_ps[(2 * c + half) % 4][:, :],
                                      b0[:, half * BANK:(half + 1) * BANK], ALU.add).then_inc(sum_read[half], 1)

            share(0)
            features(0, 3)
            share(1)
            cut(W2A + 1)
            features(0, 5)
            share(2)
            share(3)
            cut(W2A + 2)
            features(0, 7)
            gram_out(0)
            for i in (W2A + 3, W3A, W3A + 1):
                cut(i)
            pairs(0)
            dve.wait_ge(tail_in, 5 * DMA)

            def first_sums(c):
                dve.wait_ge(xp_loaded, DMA * (c + 1))
                add_bias(0, 2 * c + 1, xpart[:, 0:BANK])

            first_sums(0)
            add_bias(1, 1, xpart[:, BANK:2 * BANK])
            relu_lo(h1l[:, 0:4, :], h1h[:, 0:4, :], 0, 1)
            relu_lo(h1l[:, 4:8, :], h1h[:, 4:8, :], 1, 1)
            cut(W4)

            def second_out(c):
                relu_lo(h2l[:, 0:4, :], h2h[:, 0:4, :], 0, 2 * c + 2)
                add_bias(1, 2 * c + 2, b1[:, BANK:2 * BANK])
                relu_lo(h2l[:, 4:8, :], h2h[:, 4:8, :], 1, 3 * c + 2)

            with dve.Fori(0, CHUNKS - 1) as c:
                for g in range(1, NG, 2):
                    features(c + 1, g)
                add_bias(0, 2 * c + 2, b1[:, 0:BANK])
                gram_out(c + 1)
                second_out(c)
                pairs(c + 1)
                third_sums(c)
                first_sums(c + 1)
                relu_lo(h3l[:, :, :], h3h[:, :, :], 1, 3 * c + 3)
                add_bias(1, 2 * c + 3, xpart[:, BANK:2 * BANK])
                relu_lo(h1l[:, 0:4, :], h1h[:, 0:4, :], 0, 2 * c + 3)
                last_layer(c)
                relu_lo(h1l[:, 4:8, :], h1h[:, 4:8, :], 1, 3 * c + 4)
            c = CHUNKS - 1
            add_bias(0, 2 * c + 2, b1[:, 0:BANK])
            second_out(c)
            third_sums(c)
            relu_lo(h3l[:, :, :], h3h[:, :, :], 1, 3 * c + 3)
            last_layer(c)

        @block.tensor
        def _(pe):
            def product(dst, left, right, first, last):
                pe.matmul(dst, left[0], right[0], start=first, stop=False)
                pe.matmul(dst, left[0], right[1], start=False, stop=False)
                return pe.matmul(dst, left[1], right[0], start=False, stop=last)

            def features(c, g):
                n = GROUPS[g]
                pe.wait_ge(loaded[g], DMA * n * (c + 1))
                if g % 2 == 0:
                    pe.wait_ge(feat_even, NG // 2 * c + g // 2)
                else:
                    pe.wait_ge(feat_odd, NG // 2 * c + g // 2)
                for k in range(n):
                    t = pe.transpose(feat_ps[g % 2][:, k * P:(k + 1) * P], gat[:, FIRST[g] + k, :], ident[:, :])
                t.then_inc(turned, 1)

            def gram(c):
                pe.wait_ge(feat_x, c + 1)
                pe.wait_ge(feat_even, NG // 2 * (c + 1))
                pe.wait_ge(feat_odd, NG // 2 * (c + 1))
                for r in range(ZR):
                    if r % 2 == 0:
                        pe.wait_ge(gram_even, 2 * (ZR // 2 * c + r // 2))
                    else:
                        pe.wait_ge(gram_odd, 2 * (ZR // 2 * c + r // 2))
                    for s in range(ZS):
                        sample = feat[:, r * ZS + s, :]
                        m = pe.matmul(gram_ps[r % 2][0:NF, s * NF:(s + 1) * NF], sample, sample, start=True, stop=True)
                    m.then_inc(gram_done, 1)

            def layer(dst, h, w, cols, tiles, count):
                for k in tiles:
                    m = product(dst, (h[0][:, k, :], h[1][:, k, :]), (w[0][:, k, cols], w[1][:, k, cols]),
                                k == 0, k == count - 1)
                return m

            halves = [slice(0, BANK), slice(BANK, 2 * BANK)]

            def first_layer(half):
                layer(sum_ps[half][:, :], (rh, rl), (w1h, w1l), halves[half], range(3), 3).then_inc(sum_full[half], 1)

            def second_layer(half, tiles):
                m = layer(sum_ps[half][:, :], (h1h, h1l), (w2h, w2l), halves[half], tiles, K1)
                if K1 - 1 in tiles:
                    m.then_inc(sum_full[half], 1)

            def turn(half, src, uses):
                pe.wait_ge(turn_lo[half], 1 + uses)
                for k in range(4):
                    t = pe.transpose(turn_ps[half][:, k * P:(k + 1) * P], src[:, k * P:(k + 1) * P], ident[:, :])
                t.then_inc(turn_full[half], 1)

            def first_and_last(c, before):
                pe.wait_ge(pair_lo, c + 1)
                first_layer(0)
                if before is not None:
                    pe.wait_ge(third_read, before + 1)
                    turn(1, sums3[:, :], 3 * before + 2)
                first_layer(1)
                pe.wait_ge(sum_read[0], CHUNKS + 2 * c + 1)
                turn(0, sums[:, 0:BANK], 2 * c)
                if before is not None:
                    fourth_layer(before)
                pe.wait_ge(sum_read[1], CHUNKS + 2 * c + 1)
                turn(1, sums[:, BANK:2 * BANK], 3 * c)

            def fourth_layer(c):
                pe.wait_ge(turn_lo[1], 1 + 3 * c + 3)
                pe.wait_ge(w_lo, W4 + 1)
                layer(gram_ps[1][:, 0:n4], (h3h, h3l), (w4h, w4l), slice(0, n4), range(K3), K3).then_inc(fourth_full, 1)

            def second_and_third(c, nxt):
                pe.wait_ge(turn_lo[0], 1 + 2 * c + 1)
                for k in range(K1):
                    if k == 4:
                        pe.wait_ge(turn_lo[1], 1 + 3 * c + 1)
                    second_layer(0, range(k, k + 1))
                    if nxt is not None and k % 2 == 0:
                        features(nxt, k)
                        features(nxt, k + 1)
                if nxt is not None:
                    gram(nxt)
                    pe.wait_ge(sum_read[0], CHUNKS + 2 * c + 2)
                    turn(0, sums[:, 0:BANK], 2 * c + 1)
                    second_layer(1, range(8))
                else:
                    second_layer(1, range(4))
                    pe.wait_ge(sum_read[0], CHUNKS + 2 * c + 2)
                    turn(0, sums[:, 0:BANK], 2 * c + 1)
                    second_layer(1, range(4, 8))
                pe.wait_ge(gram_even, ZR * (c + 1 if nxt is None else c + 2))
                pe.wait_ge(turn_lo[0], 1 + 2 * c + 2)
                third = (gram_ps[0][:, :], (h2h, h2l), (w3h, w3l), slice(0, n3))
                layer(*third, range(2), K2)
                pe.wait_ge(sum_read[1], CHUNKS + 2 * c + 2)
                turn(1, sums[:, BANK:2 * BANK], 3 * c + 1)
                layer(*third, range(2, 4), K2)
                pe.wait_ge(turn_lo[1], 1 + 3 * c + 2)
                layer(*third, range(4, 8), K2).then_inc(third_full, 1)

            pe.wait_ge(ident_ready, 1)
            pe.wait_ge(chain, 4)
            by_chunk = idx_f[:, :].rearrange("f (p c) -> f c p", c=CHUNKS)
            for c in range(CHUNKS):
                t = pe.transpose(turn_ps[0][:, c * n_tab:(c + 1) * n_tab], by_chunk[:, c, :], ident[0:n_tab, 0:n_tab])
            t.then_inc(early_turned, 1)
            pe.wait_ge(den_in, DMA)
            for c in range(CHUNKS):
                t = pe.transpose(turn_ps[1][0:n_dense, c * P:(c + 1) * P], den[:, c * n_dense:(c + 1) * n_dense],
                                 ident[:, :])
            t.then_inc(early_turned, 1)
            pe.wait_ge(bias_in, 3 * DMA)
            pe.transpose(feat_ps[0][:, 0:7], brow[:, :], ident[0:7, 0:7]).then_inc(early_turned, 1)
            pe.wait_ge(turn_lo[1], 1)
            pe.wait_ge(bw0_in, DMA)
            for n in range(4):
                pe.matmul(early_ps[n][:, :], bw0s[:, n * P:(n + 1) * P], denT[:, :], start=True,
                          stop=True).then_inc(bot_full, 1)
            pe.wait_ge(bot_w_in, 2 * DMA)
            pe.wait_ge(bot_act, 2)
            pe.wait_ge(bot_dve, 2)
            for n in range(2):
                for k in range(4):
                    m = pe.matmul(early_ps[n][:, :], bw1s[:, k, n * P:(n + 1) * P], bot0[:, k, :],
                                  start=k == 0, stop=k == 3)
                m.then_inc(bot_full, 1)
                if n == 0:
                    pe.wait_ge(bcol_ready, 1)
                    features(0, 0)
            features(0, 1)
            pe.wait_ge(bot_act, 3)
            pe.wait_ge(bot_dve, 3)
            for k in range(2):
                m = pe.matmul(early_ps[2][:, :], bw2s[:, k, :], bot1[:, k, :], start=k == 0, stop=k == 1)
            m.then_inc(bot_full, 1)
            features(0, 2)
            pe.wait_ge(w_lo, W0 + 1)
            pe.wait_ge(x_lo, 1)
            for c in range(CHUNKS):
                for half in range(2):
                    if c >= 2:
                        pe.wait_ge(sum_read[half], c - 1)
                    product(early_ps[(2 * c + half) % 4][:, :], (xh[:, c * P:(c + 1) * P], xl[:, c * P:(c + 1) * P]),
                            (w0h[:, halves[half]], w0l[:, halves[half]]), True, True).then_inc(xp_full, 1)
                if c < 3:
                    features(0, 3 + c)
            features(0, 6)
            features(0, 7)
            for half in range(2):
                pe.wait_ge(sum_read[half], CHUNKS)
            gram(0)
            pe.wait_ge(w_lo, W1 + 1)
            first_and_last(0, None)
            pe.wait_ge(w_lo, W3A + 2)
            with pe.Fori(0, CHUNKS - 1) as c:
                second_and_third(c, c + 1)
                first_and_last(c + 1, c)
            second_and_third(CHUNKS - 1, None)
            pe.wait_ge(third_read, CHUNKS)
            turn(1, sums3[:, :], 3 * CHUNKS - 1)
            fourth_layer(CHUNKS - 1)


_INS = ["r_dense", "r_indices"] + ["L0_rec_" + n for n in (
    "emb_tables", "bw0", "bb0", "bw1", "bb1", "bw2", "bb2", "tw0", "tb0", "tw1", "tb1", "tw2", "tb2",
    "tw3", "tb3", "tw4", "tb4")]


def kernel(**inputs):
    import numpy as np
    import concourse.bacc as bacc
    from concourse.bass_utils import run_bass_kernel_spmd

    nc = bacc.Bacc("TRN2", target_bir_lowering=False, num_devices=1)
    arrays, args = {}, []

    def give(name, a):
        arrays[name] = a
        args.append(nc.dram_tensor(name, a.shape, mybir.dt.from_np(a.dtype), kind="ExternalInput").ap())

    for name in _INS:
        give(f"in_{name}", np.ascontiguousarray(inputs[name]))
    n_tab, vocab, emb = inputs["L0_rec_emb_tables"].shape
    give("pair_row", np.array(pair_rows(n_tab + 1, emb), np.uint32))
    give("table_base", (np.arange(n_tab, dtype=np.float32) * vocab).reshape(n_tab, 1))
    batch = inputs["r_dense"].shape[0]
    args.append(nc.dram_tensor("out_0", (batch, 1), F32, kind="ExternalOutput").ap())
    dlrm_program(nc, *args)
    r = run_bass_kernel_spmd(nc, [arrays], core_ids=[0])
    return r.results[0]["out_0"]
```

```python
from contextlib import ExitStack

import concourse.bass as bass
from concourse import mybir

ALU = mybir.AluOpType
ACT = mybir.ActivationFunctionType
F32 = mybir.dt.float32
F32R = mybir.dt.float32r
I32 = mybir.dt.int32
U32 = mybir.dt.uint32

P = 128
BANK = 512
GROUPS = (4, 3, 4, 3, 4, 3, 3, 2)
FEATURES_BEHIND = (2, 3, 4, 6)
DMA = 16


def pair_rows(n_feat, first_row):
    def row(i, j):
        a, b = min(i, j % n_feat), max(i, j % n_feat)
        return first_row + a * n_feat - a * (a + 1) // 2 + b - a - 1

    near = [[row(i, i + 1 + 3 * q + t) for t in range(3)] for i in range(n_feat) for q in range(4)]
    far = [[row(n_feat // 3 * t + r, n_feat // 3 * t + r + 13) for t in range(3)] for r in range(n_feat // 3)]
    return near + far


def dlrm_program(nc, dense, indices, tables, bw0, bb0, bw1, bb1, bw2, bb2,
                 tw0, tb0, tw1, tb1, tw2, tb2, tw3, tb3, tw4, tb4, pair_row, table_ends, out):
    B, n_dense = dense.shape
    n_tab, vocab, emb = tables.shape
    CHUNKS = B // P
    NF = n_tab + 1
    n1, n2, n3, n4 = tw0.shape[1], tw1.shape[1], tw2.shape[1], tw3.shape[1]
    U0, U1 = bw0.shape[1], bw1.shape[1]
    K1, K2, K3 = n1 // P, n2 // P, n3 // P
    HALF3 = n3 // 2
    NG = len(GROUPS)
    FIRST = [sum(GROUPS[:g]) for g in range(NG)]
    ZS = 16
    ZR = P // ZS
    JA = 14
    PK = NF * (NF - 1) // 2 // 3
    JW = NF + 13
    assert (emb, NF, n1, n2, n3, n4) == (P, 27, 1024, 1024, 512, 256) and sum(GROUPS) == n_tab

    with ExitStack() as ctx:
        def sem(name):
            return ctx.enter_context(nc.semaphore(name))

        place = [(nc.sbuf_base + 31) // 32 * 32]

        def at(name, shape, dt, offset):
            return nc.alloc_sbuf_tensor_at(name, shape, dt, offset=offset)

        def new(name, shape, dt=F32):
            size = 4
            for n in shape[1:]:
                size *= n
            offset = place[0]
            place[0] += (size + 31) // 32 * 32
            return at(name, shape, dt, offset), offset

        def parts(name, shape):
            hi, hi_at = new(name + "_hi", shape, F32R)
            lo, lo_at = new(name + "_lo", shape, F32R)
            return hi, lo, at(name + "_raw", shape, F32, lo_at), hi_at, lo_at

        w1h, w1l, w1raw, _, _ = parts("w1", [PK, 3, n1])
        w2h, w2l, w2raw, _, _ = parts("w2", [P, K1, n2])
        w3h, w3l, w3raw, w3_at, _ = parts("w3", [P, K2, n3])
        w4h, w4l, w4raw, _, _ = parts("w4", [P, K3, n4])
        feat, _ = new("feat", [P, P, NF])
        rh, _ = new("pair_hi", [PK, 3, P], F32R)
        rl, _ = new("pair_lo", [PK, 3, P], F32R)
        rraw = rl[:, :, :].bitcast(F32)
        h1h, h1_at = new("h1_hi", [P, K1, P], F32R)
        h1l, h1l_at = new("h1_lo", [P, K1, P], F32R)
        h2h, h2_at = new("h2_hi", [P, K2, P], F32R)
        h2l, h2l_at = new("h2_lo", [P, K2, P], F32R)
        h3h, h3_at = new("h3_hi", [P, K3, P], F32R)
        h3l, _ = new("h3_lo", [P, K3, P], F32R)
        gat, _ = new("gathered", [P, n_tab, emb])
        zs, zs_at = new("gram", [P, JA, P])
        xpart, _ = new("xpart", [P, n1])
        sums, _ = new("sums", [P, n1])
        sums3, _ = new("sums3", [P, n3])
        b1, _ = new("b1", [P, n2])
        b2, _ = new("b2", [P, n3])
        b3, _ = new("b3", [P, n4])
        w5, _ = new("w5", [P, n4])
        b5, _ = new("b5", [P, 1])
        xT, _ = new("xT", [P, B])
        ident, _ = new("ident", [P, P])
        rows, _ = new("rows", [P, CHUNKS * n_tab], U32)
        prow, _ = new("prow", [PK, 3], U32)
        ends, _ = new("table_ends", [n_tab, 2])
        dotc, _ = new("dotc", [P, 1])
        logit, _ = new("logit", [P, CHUNKS])
        prob, _ = new("prob", [P, CHUNKS])
        assert place[0] <= nc.sbuf_usable_end, place[0] - nc.sbuf_usable_end
        w0h = at("w0_hi", [P, n1], F32R, h1_at)
        w0l = at("w0_lo", [P, n1], F32R, h1l_at)
        w0raw = at("w0_raw", [P, n1], F32, h1l_at)
        b0 = at("b0", [P, n1], F32, h2_at)
        xh = at("x_hi", [P, B], F32R, h2l_at)
        xl = at("x_lo", [P, B], F32R, h2l_at + 4 * B)
        stage2 = at("share_stage", [P, n1], F32, h3_at)
        idx_i = at("idx_i", [n_tab, B], I32, zs_at)
        idx_n = at("idx_n", [n_tab, B], F32, zs_at + 4 * B)
        idx_f = at("idx_f", [n_tab, B], F32, zs_at + 8 * B)
        early = [w3_at]

        def new_early(name, shape, dt=F32):
            size = 4
            for n in shape[1:]:
                size *= n
            early[0] += (size + 31) // 32 * 32
            return at(name, shape, dt, early[0] - (size + 31) // 32 * 32)

        bot0 = new_early("bot0", [P, U0 // P, B])
        bot1 = new_early("bot1", [P, U1 // P, B])
        bw0s = new_early("bw0s", [n_dense, U0])
        bw1s = new_early("bw1s", [P, U0 // P, U1])
        bw2s = new_early("bw2s", [P, U1 // P, emb])
        den = new_early("den", [P, CHUNKS * n_dense])
        denT = new_early("denT", [n_dense, B])
        brow = new_early("brow", [7, P])
        bcol = new_early("bcol", [P, 7])
        stage3 = at("share_stage3", [P, n1], F32, w3_at + 4 * (2 * K2 * n3 - n1))
        assert early[0] + 4 * n1 <= w3_at + 2 * 4 * K2 * n3

        feat_ps = [ctx.enter_context(nc.psum_tensor(f"feat_ps{i}", [P, BANK], F32)) for i in range(2)]
        gram_ps = [ctx.enter_context(nc.psum_tensor(f"gram_ps{i}", [P, BANK], F32)) for i in range(2)]
        sum_ps = [ctx.enter_context(nc.psum_tensor(f"sum_ps{i}", [P, BANK], F32)) for i in range(2)]
        turn_ps = [ctx.enter_context(nc.psum_tensor(f"turn_ps{i}", [P, BANK], F32)) for i in range(2)]

        early_ps = [sum_ps[0], sum_ps[1], gram_ps[0], gram_ps[1]]
        last_third = [gram_ps[0], sum_ps[0]]
        share_ps = [gram_ps if c == 1 else sum_ps for c in range(CHUNKS)]

        GRAM = NF * (JW + 1) * P
        gram_dram = nc.dram_tensor("gram_dram", (CHUNKS * GRAM,), F32, kind="Internal").ap()
        xpart_dram = nc.dram_tensor("xpart_dram", ((CHUNKS - 1) * P * n1,), F32, kind="Internal").ap()

        idx_in, den_in, bias_in = sem("idx_in"), sem("den_in"), sem("bias_in")
        bw0_in, bot_w_in = sem("bw0_in"), sem("bot_w_in")
        prow_in, b0_in, b1_in = sem("prow_in"), sem("b0_in"), sem("b1_in")
        tail_in, b5_in = sem("tail_in"), sem("b5_in")
        w0_in, w4_in = sem("w0_in"), sem("w4_in")
        w1_in = [sem(f"w1_in{i}") for i in range(3)]
        w2_in = [sem(f"w2_in{i}") for i in range(K1 // 2)]
        w3_in = [sem(f"w3_in{i}") for i in range(K2 // 2)]
        w_hi, w_lo = sem("w_hi"), sem("w_lo")
        w4_hi, w4_lo = sem("w4_hi"), sem("w4_lo")
        ident_step, ident_ready = sem("ident_step"), sem("ident_ready")
        chain = sem("vector_chain")
        late_rows = sem("late_rows_ready")
        early_turned, bcol_ready = sem("early_turned"), sem("bcol_ready")
        bot_full = sem("bot_full")
        bot_act, bot_dve = sem("bot_read_scalar"), sem("bot_read_vector")
        x_hi, x_raw, x_lo = sem("x_hi_ready"), sem("x_ready"), sem("x_lo_ready")
        xp_full = sem("xp_full")
        xp_stored = [sem(f"xp_stored{c}") for c in range(1, CHUNKS)]
        xp_loaded = sem("xp_loaded")
        loaded = [sem(f"group_loaded{g}") for g in range(NG)]
        turned = sem("features_turned")
        feat_x, feat_even, feat_odd = sem("feat_x"), sem("feat_even"), sem("feat_odd")
        gram_done = sem("gram_done")
        gram_even, gram_odd = sem("gram_even"), sem("gram_odd")
        gram_stored, pair_loaded = sem("gram_stored"), sem("pair_loaded")
        pair_hi, pair_lo = sem("pair_hi_ready"), sem("pair_lo_ready")
        sum_full = [sem(f"sum_full{i}") for i in range(2)]
        third_full, fourth_full = sem("third_full"), sem("fourth_full")
        sum_read = [sem(f"sum_read{i}") for i in range(2)]
        third_read, fourth_read = sem("third_read"), sem("fourth_read")
        turn_full = [sem(f"turn_full{i}") for i in range(2)]
        turn_hi = [sem(f"turn_hi{i}") for i in range(2)]
        turn_lo = [sem(f"turn_lo{i}") for i in range(2)]
        dot_done, logit_done, prob_done, out_done = (
            sem("dot_done"), sem("logit_done"), sem("prob_done"), sem("out_done"))

        W0, W1, W2 = 0, 1, 2
        W1_REST, W3 = W2 + K1, W2 + K1 + 2
        piece = [(w0h[:, :], w0l[:, :], w0raw[:, :], w0_in)]
        first = [(w1h[:, t, :], w1l[:, t, :], w1raw[:, t, :], w1_in[t]) for t in range(3)]
        piece += first[0:1]
        piece += [(w2h[:, k, :], w2l[:, k, :], w2raw[:, k, :], w2_in[k // 2]) for k in range(K1)]
        piece += first[1:3]
        piece += [(w3h[:, k:k + 2, :], w3l[:, k:k + 2, :], w3raw[:, k:k + 2, :], w3_in[k // 2]) for k in range(0, K2, 2)]

        block = ctx.enter_context(nc.Block())

        @block.gpsimd
        def _(pool):
            pool.memset(ident[:, :], 0.0).then_inc(ident_step, 1)
            pool.wait_ge(ident_step, 1)
            pool.affine_select(out=ident[:, :], in_=ident[:, :], compare_op=ALU.not_equal, fill=1.0,
                               base=0, pattern=[[-1, P]], channel_multiplier=1).then_inc(ident_ready, 1)
            pool.wait_ge(prow_in, DMA)

            def gather_w1(t):
                pool.indirect_dma_start(
                    out=w1raw[:, t, :], out_offset=None, in_=tw0,
                    in_offset=bass.IndirectOffsetOnAxis(ap=prow[:, t:t + 1], axis=0),
                ).then_inc(w1_in[t], DMA)

            gather_w1(0)
            pool.wait_ge(turn_lo[0], 1)
            all_rows = tables.rearrange("t v e -> (t v) e")
            for c in range(CHUNKS):
                if c == 1:
                    gather_w1(1)
                    gather_w1(2)
                    pool.wait_ge(late_rows, 1)
                if c == 2:
                    pool.wait_ge(w4_in, DMA)
                    pool.tensor_copy(w4h[:, :, :], w4raw[:, :, :]).then_inc(w4_hi, 1)
                    pool.wait_ge(w4_hi, 1)
                    pool.tensor_tensor(w4l[:, :, :], w4raw[:, :, :], w4h[:, :, :].bitcast(F32),
                                       ALU.subtract).then_inc(w4_lo, 1)
                for g, size in enumerate(GROUPS):
                    if c > 0:
                        pool.wait_ge(turned, NG * (c - 1) + g + 1)
                    for k in range(FIRST[g], FIRST[g] + size):
                        col = c * n_tab + k
                        pool.indirect_dma_start(
                            out=gat[:, k, :], out_offset=None, in_=all_rows,
                            in_offset=bass.IndirectOffsetOnAxis(ap=rows[:, col:col + 1], axis=0),
                        ).then_inc(loaded[g], DMA)

        @block.sync
        def _(sp):
            sp.dma_start(idx_i[:, :], indices).then_inc(idx_in, DMA)
            sp.dma_start(ends[:, :], table_ends).then_inc(idx_in, DMA)
            sp.dma_start(prow[:, :], pair_row).then_inc(prow_in, DMA)
            sp.dma_start(den[:, :], dense.rearrange("(p c) k -> p (c k)", c=CHUNKS)).then_inc(den_in, DMA)
            sp.dma_start(bw0s[:, :], bw0).then_inc(bw0_in, DMA)
            sp.dma_start(brow[0:4, :], bb0.rearrange("(m p) -> m p", p=P)).then_inc(bias_in, DMA)
            sp.dma_start(brow[4:6, :], bb1.rearrange("(m p) -> m p", p=P)).then_inc(bias_in, DMA)
            sp.dma_start(brow[6:7, :], bb2.rearrange("(m p) -> m p", p=P)).then_inc(bias_in, DMA)
            sp.dma_start(bw1s[:, :, :], bw1.rearrange("(k p) n -> p k n", p=P)).then_inc(bot_w_in, DMA)
            sp.dma_start(bw2s[:, :, :], bw2.rearrange("(k p) n -> p k n", p=P)).then_inc(bot_w_in, DMA)
            sp.dma_start(w0raw[:, :], tw0[0:P, :]).then_inc(w0_in, DMA)
            sp.dma_start(b0[:, :], tb0.partition_broadcast(P)).then_inc(b0_in, DMA)
            w2_rows = tw1.rearrange("(k p) n -> p k n", p=P)
            w3_rows = tw2.rearrange("(k p) n -> p k n", p=P)

            def behind(g):
                sp.wait_ge(loaded[g], DMA * GROUPS[g])

            def load_w2(i):
                sp.dma_start(w2raw[:, 2 * i:2 * i + 2, :], w2_rows[:, 2 * i:2 * i + 2, :]).then_inc(w2_in[i], DMA)

            def load_w3(i):
                sp.dma_start(w3raw[:, 2 * i:2 * i + 2, :], w3_rows[:, 2 * i:2 * i + 2, :]).then_inc(w3_in[i], DMA)

            def store_share(c, stage):
                sp.wait_ge(sum_read[0], c + 1)
                sp.wait_ge(sum_read[1], c + 1)
                sp.dma_start(xpart_dram[(c - 1) * P * n1:c * P * n1].rearrange("(p n) -> p n", p=P),
                             stage[:, :]).then_inc(xp_stored[c - 1], DMA)

            behind(0)
            load_w2(0)
            behind(1)
            load_w2(1)
            behind(2)
            load_w2(2)
            behind(3)
            load_w2(3)
            behind(5)
            store_share(1, sums)
            behind(7)
            sp.wait_ge(bot_full, 7)
            sp.wait_ge(x_hi, 1)
            sp.wait_ge(x_raw, 1)
            load_w3(0)
            load_w3(1)

            def pairs_through_dram(start, copied, stored):
                flat = gram_dram[bass.ds(start, GRAM)]
                by_row = flat[0:NF * JW * P].rearrange("(i j b) -> i j b", i=NF, j=JW)
                skewed = flat.rearrange("(i j b) -> i j b", i=NF, j=JW + 1)
                sp.wait_ge(gram_even, copied)
                sp.wait_ge(gram_odd, copied)
                sp.dma_start(by_row[:, JA:NF, :], zs[32:32 + NF, 0:NF - JA, :]).then_inc(gram_stored, DMA)
                sp.dma_start(by_row[0:13, 1:JA, :], zs[0:13, 1:JA, :]).then_inc(gram_stored, DMA)
                sp.dma_start(by_row[14:NF, NF:JW, :], zs[14:NF, 0:13, :]).then_inc(gram_stored, DMA)
                sp.wait_ge(gram_stored, stored)
                sp.dma_start(rraw[0:4 * NF, :, :].rearrange("p t b -> p (t b)"),
                             skewed[:, 1:13, :].rearrange("i (q t) b -> i q (t b)", q=4)).then_inc(pair_loaded, DMA)
                sp.dma_start(rraw[4 * NF:PK, :, :],
                             skewed[:, 13, :].rearrange("(t r) b -> r t b", t=3)).then_inc(pair_loaded, DMA)

            pairs_through_dram(0, ZR, 3 * DMA)
            store_share(2, stage2)
            store_share(3, stage3)
            load_w3(2)
            sp.wait_ge(xp_stored[2], DMA)
            load_w3(3)
            sp.dma_start(b1[:, :], tb1.partition_broadcast(P)).then_inc(b1_in, DMA)
            sp.dma_start(w4raw[:, :, :], tw3.rearrange("(k p) n -> p k n", p=P)).then_inc(w4_in, DMA)
            sp.dma_start(b2[:, :], tb2.partition_broadcast(P)).then_inc(tail_in, DMA)
            sp.dma_start(b3[:, :], tb3.partition_broadcast(P)).then_inc(tail_in, DMA)
            sp.dma_start(w5[:, :], tw4.rearrange("n o -> (n o)").partition_broadcast(P)).then_inc(tail_in, DMA)
            sp.dma_start(b5[:, :], tb4.partition_broadcast(P)).then_inc(b5_in, DMA)
            for stored in xp_stored:
                sp.wait_ge(stored, DMA)
            with sp.Fori(0, CHUNKS - 1) as c:
                shared = sp.snap(2 * c + CHUNKS + 1)
                copied = sp.snap(ZR * c + 2 * ZR)
                stored = sp.snap(3 * DMA * c + 6 * DMA)
                xpart_at = sp.snap(c * (P * n1))
                gram_at = sp.snap((c + 1) * GRAM)
                sp.wait_ge(sum_read[0], shared)
                sp.wait_ge(sum_read[1], shared)
                sp.dma_start(xpart[:, :], xpart_dram[bass.ds(xpart_at, P * n1)].rearrange("(p n) -> p n", p=P)).then_inc(xp_loaded, DMA)
                pairs_through_dram(gram_at, copied, stored)
            sp.wait_ge(prob_done, 2)
            sp.dma_start(out.rearrange("(p c) o -> p (c o)", c=CHUNKS), prob[:, :]).then_inc(out_done, DMA)
            sp.wait_ge(out_done, DMA)

        @block.scalar
        def _(act):
            def cut(i):
                act.wait_ge(piece[i][3], DMA)
                act.activation(piece[i][0], piece[i][2], ACT.Copy).then_inc(w_hi, 1)

            def bottom_feature(c):
                act.wait_ge(gram_done, ZR * c)
                act.activation(feat[:, :, 0], xT[:, bass.ds(c * P, P)], ACT.Copy).then_inc(feat_x, 1)

            def features(c, g):
                n = GROUPS[g]
                act.wait_ge(turned, NG * c + g + 1)
                act.activation(feat[:, :, 1 + FIRST[g]:1 + FIRST[g] + n],
                               feat_ps[0][:, 0:n * P].rearrange("p (f b) -> p b f", f=n),
                               ACT.Copy).then_inc(feat_even, 1)

            def gram_out(c):
                act.wait_ge(gram_stored, 3 * DMA * c)
                for r in range(0, ZR, 2):
                    act.wait_ge(gram_done, ZR * c + r + 1)
                    table = gram_ps[0][0:NF, 0:ZS * NF].rearrange("p (s j) -> p j s", s=ZS)
                    act.activation(zs[0:NF, 0:JA, r * ZS:(r + 1) * ZS], table[:, 0:JA, :],
                                   ACT.Copy).then_inc(gram_even, 1)
                    act.activation(zs[32:32 + NF, 0:NF - JA, r * ZS:(r + 1) * ZS], table[:, JA:NF, :],
                                   ACT.Copy).then_inc(gram_even, 1)

            def pairs(c):
                act.wait_ge(pair_loaded, 2 * DMA * (c + 1))
                act.activation(rh[:, :, :], rraw[:, :, :], ACT.Copy).then_inc(pair_hi, 1)

            def relu_hi(dst, half, count, width=BANK):
                act.wait_ge(turn_full[half], count)
                act.activation(dst, turn_ps[half][:, 0:width].rearrange("p (k b) -> p k b", b=P),
                               ACT.Relu).then_inc(turn_hi[half], 1)

            def bottom_relu(n, dst):
                act.wait_ge(bot_full, n + 1)
                act.activation(dst, early_ps[n % 4][:, :], ACT.Relu, bias=bcol[:, n:n + 1]).then_inc(bot_act, 1)

            act.wait_ge(early_turned, 4)
            act.activation(bcol[:, :], feat_ps[0][:, 0:7], ACT.Copy).then_inc(bcol_ready, 1)
            act.wait_ge(bcol_ready, 1)
            bottom_relu(0, bot0[:, 0, :])
            bottom_relu(2, bot0[:, 2, :])
            cut(W0)
            cut(W1)
            bottom_relu(4, bot1[:, 0, :])
            cut(W2)
            cut(W2 + 1)
            cut(W2 + 2)
            act.wait_ge(bot_full, 7)
            act.activation(xh[:, :], early_ps[2][:, :], ACT.Relu, bias=bcol[:, 6:7]).then_inc(x_hi, 1)
            features(0, 0)
            act.wait_ge(x_raw, 1)
            act.activation(feat[:, :, 0], xT[:, 0:P], ACT.Copy).then_inc(feat_x, 1)
            cut(W2 + 3)
            cut(W2 + 4)
            features(0, 2)
            cut(W2 + 5)
            features(0, 4)
            cut(W2 + 6)
            cut(W2 + 7)
            features(0, 6)
            gram_out(0)
            for i in range(W1_REST, W3 + 2):
                cut(i)
            pairs(0)
            relu_hi(h1h[:, 0:4, :], 0, 1)
            relu_hi(h1h[:, 4:8, :], 1, 1)
            cut(W3 + 2)
            cut(W3 + 3)

            def second_out(c):
                relu_hi(h2h[:, 0:4, :], 0, 2 * c + 2)
                relu_hi(h2h[:, 4:8, :], 1, 3 * c + 2)

            with act.Fori(0, CHUNKS - 1) as c:
                bottom_feature(c + 1)
                for g in range(0, NG, 2):
                    features(c + 1, g)
                gram_out(c + 1)
                second_out(c)
                pairs(c + 1)
                relu_hi(h3h[:, :, :], 1, 3 * c + 3)
                relu_hi(h1h[:, 0:4, :], 0, 2 * c + 3)
                relu_hi(h1h[:, 4:8, :], 1, 3 * c + 4)
            second_out(CHUNKS - 1)
            relu_hi(h3h[:, 0:2, :], 1, 3 * CHUNKS, HALF3)
            relu_hi(h3h[:, 2:4, :], 0, 2 * CHUNKS + 1, HALF3)
            act.wait_ge(b5_in, DMA)
            for cols, chunks in ((slice(0, CHUNKS - 1), CHUNKS - 1), (slice(CHUNKS - 1, CHUNKS), CHUNKS)):
                act.wait_ge(logit_done, chunks)
                act.activation(prob[:, cols], logit[:, cols], ACT.Sigmoid, bias=b5[:, 0:1]).then_inc(prob_done, 1)

        @block.vector
        def _(dve):
            def cut(i):
                dve.wait_ge(w_hi, i + 1)
                dve.tensor_tensor(piece[i][1], piece[i][2], piece[i][0].bitcast(F32), ALU.subtract).then_inc(w_lo, 1)

            def features(c, g):
                n = GROUPS[g]
                dve.wait_ge(turned, NG * c + g + 1)
                dve.tensor_copy(feat[:, :, 1 + FIRST[g]:1 + FIRST[g] + n],
                                feat_ps[1][:, 0:n * P].rearrange("p (f b) -> p b f", f=n)).then_inc(feat_odd, 1)

            def gram_out(c, cuts=()):
                dve.wait_ge(gram_stored, 3 * DMA * c)
                for r in range(1, ZR, 2):
                    dve.wait_ge(gram_done, ZR * c + r + 1)
                    table = gram_ps[1][0:NF, 0:ZS * NF].rearrange("p (s j) -> p j s", s=ZS)
                    dve.tensor_copy(zs[0:NF, 0:JA, r * ZS:(r + 1) * ZS], table[:, 0:JA, :]).then_inc(gram_odd, 1)
                    dve.tensor_copy(zs[32:32 + NF, 0:NF - JA, r * ZS:(r + 1) * ZS],
                                    table[:, JA:NF, :]).then_inc(gram_odd, 1)
                    for i in cuts[r // 2:r // 2 + 1]:
                        cut(i)

            def pairs(c):
                dve.wait_ge(pair_hi, c + 1)
                dve.tensor_tensor(rl[:, :, :], rraw[:, :, :], rh[:, :, :].bitcast(F32), ALU.subtract).then_inc(pair_lo, 1)

            def add_bias(half, count, bias):
                dve.wait_ge(sum_full[half], count)
                dve.tensor_tensor(sums[:, half * BANK:(half + 1) * BANK], sum_ps[half][:, :], bias,
                                  ALU.add).then_inc(sum_read[half], 1)

            def relu_lo(dst, hi, half, count, width=BANK):
                dve.wait_ge(turn_hi[half], count)
                dve.scalar_tensor_tensor(out=dst, in0=turn_ps[half][:, 0:width].rearrange("p (k b) -> p k b", b=P),
                                         scalar=0.0, in1=hi.bitcast(F32), op0=ALU.max,
                                         op1=ALU.subtract).then_inc(turn_lo[half], 1)

            def third_sums(c):
                dve.wait_ge(tail_in, 3 * DMA)
                dve.wait_ge(xp_stored[1], DMA)
                dve.wait_ge(third_full, c + 1)
                dve.tensor_tensor(sums3[:, :], gram_ps[0][:, :], b2[:, :], ALU.add).then_inc(third_read, 1)

            def last_layer(c):
                dve.wait_ge(fourth_full, c + 1)
                dve.tensor_tensor(sums3[:, 0:n4], gram_ps[1][:, 0:n4], b3[:, :], ALU.add).then_inc(fourth_read, 1)
                dve.wait_ge(fourth_read, c + 1)
                last = isinstance(c, int)
                dot = logit[:, c:c + 1] if last else dotc[:, :]
                dve.scalar_tensor_tensor(out=sums3[:, n4:2 * n4], in0=sums3[:, 0:n4], scalar=0.0,
                                         in1=w5[:, :], op0=ALU.max, op1=ALU.mult,
                                         accum_out=dot).then_inc(logit_done if last else dot_done, 1)
                if last:
                    return
                dve.wait_ge(dot_done, c + 1)
                dve.tensor_copy(logit[:, bass.ds(c, 1)], dotc[:, :]).then_inc(logit_done, 1)

            steps = [0]

            def link(ins):
                steps[0] += 1
                ins.then_inc(chain, 1)
                dve.wait_ge(chain, steps[0])

            dve.wait_ge(idx_in, 2 * DMA)
            given, wrapped, row = (x[:, :].rearrange("f (p c) -> f c p", c=CHUNKS) for x in (idx_i, idx_n, idx_f))
            first_chunk, later_chunks = slice(0, 1), slice(1, CHUNKS)
            for cs in (first_chunk, later_chunks):
                link(dve.tensor_scalar(wrapped[:, cs, :], given[:, cs, :], 0.0, float(vocab), ALU.is_lt, ALU.mult))
                link(dve.scalar_tensor_tensor(out=row[:, cs, :], in0=wrapped[:, cs, :], scalar=ends[:, 0:1],
                                              in1=given[:, cs, :], op0=ALU.add, op1=ALU.add))
                link(dve.tensor_scalar(row[:, cs, :], row[:, cs, :], ends[:, 0:1], ends[:, 1:2], ALU.max, ALU.min))
                if cs == first_chunk:
                    dve.wait_ge(early_turned, 1)
                    dve.tensor_copy(rows[:, 0:n_tab], turn_ps[0][:, 0:n_tab]).then_inc(turn_lo[0], 1)
            dve.wait_ge(early_turned, 2)
            dve.tensor_copy(denT[:, :], turn_ps[1][0:n_dense, :]).then_inc(turn_lo[1], 1)
            dve.wait_ge(early_turned, 3)
            dve.tensor_copy(rows[:, n_tab:CHUNKS * n_tab],
                            gram_ps[1][:, 0:(CHUNKS - 1) * n_tab]).then_inc(late_rows, 1)
            dve.wait_ge(bcol_ready, 1)

            def bottom_relu(n, dst):
                dve.wait_ge(bot_full, n + 1)
                return dve.tensor_scalar(dst, early_ps[n % 4][:, :], bcol[:, n:n + 1], 0.0, ALU.add, ALU.max)

            bottom_relu(1, bot0[:, 1, :]).then_inc(bot_dve, 1)
            bottom_relu(3, bot0[:, 3, :]).then_inc(bot_dve, 1)
            cut(W0)
            cut(W1)
            bottom_relu(5, bot1[:, 1, :]).then_inc(bot_dve, 1)
            cut(W2)
            cut(W2 + 1)
            dve.wait_ge(x_hi, 1)
            bottom_relu(6, xT[:, :]).then_inc(x_raw, 1)
            dve.wait_ge(x_raw, 1)
            dve.tensor_tensor(xl[:, :], xT[:, :], xh[:, :].bitcast(F32), ALU.subtract).then_inc(x_lo, 1)
            features(0, 1)
            dve.wait_ge(b0_in, DMA)

            def share(c, stage):
                for half in range(2):
                    dve.wait_ge(xp_full, 2 * c + half + 1)
                    dve.tensor_tensor(stage[:, half * BANK:(half + 1) * BANK], share_ps[c][half][:, :],
                                      b0[:, half * BANK:(half + 1) * BANK], ALU.add).then_inc(sum_read[half], 1)

            share(0, xpart)
            share(1, sums)
            features(0, 3)
            share(2, stage2)
            features(0, 5)
            share(3, stage3)
            cut(W2 + 2)
            features(0, 7)
            cut(W2 + 3)
            gram_out(0, (W2 + 4, W2 + 5, W2 + 6))
            for i in range(W2 + 7, W3 + 2):
                cut(i)
            pairs(0)

            dve.wait_ge(xp_stored[0], DMA)
            add_bias(0, 1, xpart[:, 0:BANK])
            add_bias(1, 1, xpart[:, BANK:2 * BANK])
            relu_lo(h1l[:, 0:4, :], h1h[:, 0:4, :], 0, 1)
            relu_lo(h1l[:, 4:8, :], h1h[:, 4:8, :], 1, 1)
            cut(W3 + 2)
            cut(W3 + 3)

            def second_out(c):
                relu_lo(h2l[:, 0:4, :], h2h[:, 0:4, :], 0, 2 * c + 2)
                add_bias(1, 2 * c + 2, b1[:, BANK:2 * BANK])
                relu_lo(h2l[:, 4:8, :], h2h[:, 4:8, :], 1, 3 * c + 2)

            with dve.Fori(0, CHUNKS - 1) as c:
                for g in range(1, NG, 2):
                    features(c + 1, g)
                dve.wait_ge(b1_in, DMA)
                add_bias(0, 2 * c + 2, b1[:, 0:BANK])
                gram_out(c + 1)
                second_out(c)
                pairs(c + 1)
                third_sums(c)
                dve.wait_ge(xp_loaded, DMA * (c + 1))
                add_bias(0, 2 * c + 3, xpart[:, 0:BANK])
                relu_lo(h3l[:, :, :], h3h[:, :, :], 1, 3 * c + 3)
                add_bias(1, 2 * c + 3, xpart[:, BANK:2 * BANK])
                relu_lo(h1l[:, 0:4, :], h1h[:, 0:4, :], 0, 2 * c + 3)
                last_layer(c)
                relu_lo(h1l[:, 4:8, :], h1h[:, 4:8, :], 1, 3 * c + 4)
            c = CHUNKS - 1
            add_bias(0, 2 * c + 2, b1[:, 0:BANK])
            second_out(c)
            for j in range(2):
                cols = slice(j * HALF3, (j + 1) * HALF3)
                dve.wait_ge(third_full, CHUNKS + j)
                dve.tensor_tensor(sums3[:, cols], last_third[j][:, 0:HALF3], b2[:, cols], ALU.add).then_inc(third_read, 1)
            relu_lo(h3l[:, 0:2, :], h3h[:, 0:2, :], 1, 3 * CHUNKS, HALF3)
            relu_lo(h3l[:, 2:4, :], h3h[:, 2:4, :], 0, 2 * CHUNKS + 1, HALF3)
            last_layer(c)

        @block.tensor
        def _(pe):
            def product(dst, left, right, first, last):
                pe.matmul(dst, left[0], right[0], start=first, stop=False)
                pe.matmul(dst, left[0], right[1], start=False, stop=False)
                return pe.matmul(dst, left[1], right[0], start=False, stop=last)

            def features(c, g):
                n = GROUPS[g]
                pe.wait_ge(loaded[g], DMA * n * (c + 1))
                if g % 2 == 0:
                    pe.wait_ge(feat_even, NG // 2 * c + g // 2)
                else:
                    pe.wait_ge(feat_odd, NG // 2 * c + g // 2)
                for k in range(n):
                    t = pe.transpose(feat_ps[g % 2][:, k * P:(k + 1) * P], gat[:, FIRST[g] + k, :], ident[:, :])
                t.then_inc(turned, 1)

            def gram(c):
                pe.wait_ge(feat_x, c + 1)
                pe.wait_ge(feat_even, NG // 2 * (c + 1))
                pe.wait_ge(feat_odd, NG // 2 * (c + 1))
                for r in range(ZR):
                    if r % 2 == 0:
                        pe.wait_ge(gram_even, 2 * (ZR // 2 * c + r // 2))
                    else:
                        pe.wait_ge(gram_odd, 2 * (ZR // 2 * c + r // 2))
                    for s in range(ZS):
                        sample = feat[:, r * ZS + s, :]
                        m = pe.matmul(gram_ps[r % 2][0:NF, s * NF:(s + 1) * NF], sample, sample, start=True, stop=True)
                    m.then_inc(gram_done, 1)

            def layer(dst, h, w, cols, steps, count):
                for step in steps:
                    k, part = divmod(step, 3)
                    m = pe.matmul(dst, h[part == 2][:, k, :], w[part == 1][:, k, cols],
                                  start=step == 0, stop=step == 3 * count - 1)
                return m

            halves = [slice(0, BANK), slice(BANK, 2 * BANK)]

            def first_layer(half, c=None):
                for t in range(3):
                    w = (w1h[:, t, halves[half]], w1l[:, t, halves[half]])
                    pe.matmul(sum_ps[half][:, :], rh[:, t, :], w[0], start=t == 0, stop=False)
                    pe.matmul(sum_ps[half][:, :], rh[:, t, :], w[1], start=False, stop=False)
                if c is not None:
                    pe.wait_ge(pair_lo, c + 1)
                for t in range(3):
                    m = pe.matmul(sum_ps[half][:, :], rl[:, t, :], w1h[:, t, halves[half]], start=False, stop=t == 2)
                m.then_inc(sum_full[half], 1)

            def second_layer(half, first, end):
                m = layer(sum_ps[half][:, :], (h1h, h1l), (w2h, w2l), halves[half], range(3 * first, 3 * end), K1)
                if end == K1:
                    m.then_inc(sum_full[half], 1)

            def turn(half, src, uses, tiles=4):
                pe.wait_ge(turn_lo[half], 1 + uses)
                for k in range(tiles):
                    t = pe.transpose(turn_ps[half][:, k * P:(k + 1) * P], src[:, k * P:(k + 1) * P], ident[:, :])
                t.then_inc(turn_full[half], 1)

            def first_and_last(c, before):
                pe.wait_ge(pair_hi, c + 1)
                first_layer(0, c)
                if before is not None:
                    pe.wait_ge(third_read, before + 1)
                    turn(1, sums3[:, :], 3 * before + 2)
                first_layer(1)
                pe.wait_ge(sum_read[0], CHUNKS + 2 * c + 1)
                turn(0, sums[:, 0:BANK], 2 * c)
                if before is not None:
                    fourth_layer(before)
                pe.wait_ge(sum_read[1], CHUNKS + 2 * c + 1)
                turn(1, sums[:, BANK:2 * BANK], 3 * c)

            def fourth_steps(first, end):
                return layer(gram_ps[1][:, 0:n4], (h3h, h3l), (w4h, w4l), slice(0, n4), range(first, end), K3)

            def fourth_layer(c):
                pe.wait_ge(turn_lo[1], 1 + 3 * c + 3)
                pe.wait_ge(w4_lo, 1)
                fourth_steps(0, 3 * K3).then_inc(fourth_full, 1)

            def second_and_third(c, nxt):
                pe.wait_ge(turn_lo[0], 1 + 2 * c + 1)
                for k in range(K1):
                    if k == 4:
                        pe.wait_ge(turn_lo[1], 1 + 3 * c + 1)
                    second_layer(0, k, k + 1)
                    if nxt is not None and k in FEATURES_BEHIND:
                        pair = FEATURES_BEHIND.index(k)
                        features(nxt, 2 * pair)
                        features(nxt, 2 * pair + 1)
                if nxt is not None:
                    gram(nxt)
                    pe.wait_ge(sum_read[0], CHUNKS + 2 * c + 2)
                    turn(0, sums[:, 0:BANK], 2 * c + 1)
                    second_layer(1, 0, 8)
                else:
                    second_layer(1, 0, 4)
                    pe.wait_ge(sum_read[0], CHUNKS + 2 * c + 2)
                    turn(0, sums[:, 0:BANK], 2 * c + 1)
                    second_layer(1, 4, 8)
                pe.wait_ge(w_lo, W3 + 4)
                pe.wait_ge(gram_even, ZR * (c + 1 if nxt is None else c + 2))
                pe.wait_ge(turn_lo[0], 1 + 2 * c + 2)

                def third_layer(first, end):
                    if nxt is not None:
                        return layer(gram_ps[0][:, :], (h2h, h2l), (w3h, w3l), slice(0, n3), range(first, end), K2)
                    for j in range(2):
                        third_half(j, first, end)

                third_layer(0, 4)
                pe.wait_ge(sum_read[1], CHUNKS + 2 * c + 2)
                turn(1, sums[:, BANK:2 * BANK], 3 * c + 1)
                third_layer(4, 3 * K2 // 2)
                pe.wait_ge(turn_lo[1], 1 + 3 * c + 2)
                if nxt is not None:
                    third_layer(3 * K2 // 2, 3 * K2).then_inc(third_full, 1)

            def third_half(j, first, end):
                return layer(last_third[j][:, 0:HALF3], (h2h, h2l), (w3h, w3l),
                             slice(j * HALF3, (j + 1) * HALF3), range(first, end), K2)

            def keep_warm(n, bank):
                for _ in range(n):
                    pe.transpose(bank[:, 0:P], ident[:, :], ident[:, :])

            pe.wait_ge(ident_ready, 1)
            keep_warm(12, feat_ps[1])
            pe.wait_ge(chain, 3)
            by_chunk = idx_f[:, :].rearrange("f (p c) -> f c p", c=CHUNKS)
            pe.transpose(turn_ps[0][:, 0:n_tab], by_chunk[:, 0, :], ident[0:n_tab, 0:n_tab]).then_inc(early_turned, 1)
            pe.wait_ge(den_in, DMA)
            for c in range(CHUNKS):
                t = pe.transpose(turn_ps[1][0:n_dense, c * P:(c + 1) * P], den[:, c * n_dense:(c + 1) * n_dense],
                                 ident[:, :])
            t.then_inc(early_turned, 1)
            keep_warm(5, feat_ps[1])
            pe.wait_ge(chain, 6)
            for c in range(1, CHUNKS):
                t = pe.transpose(gram_ps[1][:, (c - 1) * n_tab:c * n_tab], by_chunk[:, c, :], ident[0:n_tab, 0:n_tab])
            t.then_inc(early_turned, 1)
            pe.wait_ge(bias_in, 3 * DMA)
            pe.transpose(feat_ps[0][:, 0:7], brow[:, :], ident[0:7, 0:7]).then_inc(early_turned, 1)
            pe.wait_ge(turn_lo[1], 1)
            pe.wait_ge(bw0_in, DMA)
            for n in range(4):
                if n == 3:
                    pe.wait_ge(late_rows, 1)
                pe.matmul(early_ps[n][:, :], bw0s[:, n * P:(n + 1) * P], denT[:, :], start=True,
                          stop=True).then_inc(bot_full, 1)
            pe.wait_ge(turn_lo[0], 1)
            keep_warm(9, turn_ps[0])
            pe.wait_ge(bot_w_in, 2 * DMA)
            pe.wait_ge(bot_act, 2)
            pe.wait_ge(bot_dve, 2)
            for n in range(2):
                for k in range(4):
                    m = pe.matmul(early_ps[n][:, :], bw1s[:, k, n * P:(n + 1) * P], bot0[:, k, :],
                                  start=k == 0, stop=k == 3)
                m.then_inc(bot_full, 1)
            pe.wait_ge(bot_act, 3)
            pe.wait_ge(bot_dve, 3)
            for k in range(2):
                m = pe.matmul(early_ps[2][:, :], bw2s[:, k, :], bot1[:, k, :], start=k == 0, stop=k == 1)
            m.then_inc(bot_full, 1)
            pe.wait_ge(bcol_ready, 1)
            features(0, 0)
            features(0, 1)

            def share(c):
                if c >= 2:
                    for half in range(2):
                        pe.wait_ge(sum_read[half], 1 if c == 2 else 3)
                x = (xh[:, c * P:(c + 1) * P], xl[:, c * P:(c + 1) * P])
                for half in range(2):
                    product(share_ps[c][half][:, :], x, (w0h[:, halves[half]], w0l[:, halves[half]]),
                            True, True).then_inc(xp_full, 1)

            pe.wait_ge(w_lo, W0 + 1)
            pe.wait_ge(x_lo, 1)
            share(0)
            features(0, 2)
            share(1)
            features(0, 3)
            share(2)
            features(0, 4)
            features(0, 5)
            share(3)
            keep_warm(10, turn_ps[0])
            features(0, 6)
            features(0, 7)
            for half in range(2):
                pe.wait_ge(sum_read[half], 2)
            gram(0)
            keep_warm(62, turn_ps[0])
            pe.wait_ge(w_lo, W1_REST + 2)
            for half in range(2):
                pe.wait_ge(sum_read[half], CHUNKS)
            first_and_last(0, None)
            with pe.Fori(0, CHUNKS - 1) as c:
                second_and_third(c, c + 1)
                first_and_last(c + 1, c)
            second_and_third(CHUNKS - 1, None)
            third_half(0, 12, 24).then_inc(third_full, 1)
            third_half(1, 12, 18)
            pe.wait_ge(third_read, CHUNKS)
            turn(1, sums3[:, 0:HALF3], 3 * CHUNKS - 1, 2)
            third_half(1, 18, 24).then_inc(third_full, 1)
            pe.wait_ge(third_read, CHUNKS + 1)
            turn(0, sums3[:, HALF3:2 * HALF3], 2 * CHUNKS, 2)
            pe.wait_ge(turn_lo[1], 1 + 3 * CHUNKS)
            fourth_steps(0, 3 * K3 // 2)
            pe.wait_ge(turn_lo[0], 1 + 2 * CHUNKS + 1)
            fourth_steps(3 * K3 // 2, 3 * K3).then_inc(fourth_full, 1)


_INS = ["r_dense", "r_indices"] + ["L0_rec_" + n for n in (
    "emb_tables", "bw0", "bb0", "bw1", "bb1", "bw2", "bb2", "tw0", "tb0", "tw1", "tb1", "tw2", "tb2",
    "tw3", "tb3", "tw4", "tb4")]


def kernel(**inputs):
    import numpy as np
    import concourse.bacc as bacc
    from concourse.bass_utils import run_bass_kernel_spmd

    nc = bacc.Bacc("TRN2", target_bir_lowering=False, num_devices=1)
    arrays, args = {}, []

    def give(name, a):
        arrays[name] = a
        args.append(nc.dram_tensor(name, a.shape, mybir.dt.from_np(a.dtype), kind="ExternalInput").ap())

    for name in _INS:
        give(f"in_{name}", np.ascontiguousarray(inputs[name]))
    n_tab, vocab, emb = inputs["L0_rec_emb_tables"].shape
    give("pair_row", np.array(pair_rows(n_tab + 1, emb), np.uint32))
    first_rows = np.arange(n_tab, dtype=np.float32) * vocab
    give("table_ends", np.stack([first_rows, first_rows + vocab - 1], axis=1))
    batch = inputs["r_dense"].shape[0]
    args.append(nc.dram_tensor("out_0", (batch, 1), F32, kind="ExternalOutput").ap())
    dlrm_program(nc, *args)
    r = run_bass_kernel_spmd(nc, [arrays], core_ids=[0])
    return r.results[0]["out_0"]
```
